# Optimizing a Trainium2 kernel written in Bass

```python
import numpy as np
import jax
import jax.numpy as jnp

def _softmax(x, axis=-1):
    return jax.nn.softmax(x, axis=axis)

def _gelu(x):
    return jax.nn.gelu(x, approximate=True)

def _silu(x):
    return jax.nn.silu(x)

def _sigmoid(x):
    return jax.nn.sigmoid(x)

def _layernorm(x, axis=-1, eps=1e-05):
    m = jnp.mean(x, axis=axis, keepdims=True)
    v = jnp.var(x, axis=axis, keepdims=True)
    return (x - m) / jnp.sqrt(v + eps)

def _scatter_add(tgt, idx, src, axis=0):
    return tgt.at[idx].add(src)

def _segment_sum(src, seg, n):
    return jax.ops.segment_sum(src, seg, n)
kernel_name = 'mk_gnn_resnorm_d2_gnn_r32_b0149e'

def setup_inputs(seed: int=0):
    np.random.seed(seed)
    _w = jnp.asarray

    def _rec_inputs():
        import jax
        import jax.numpy as jnp
        _gk = jax.random.key(seed)
        x = -0.0005121 + 1.001 * jax.random.normal(jax.random.fold_in(_gk, 1), (3125, 64), jnp.float32)
        _s = jax.random.randint(jax.random.fold_in(_gk, 2), (50000,), 0, 3125, jnp.int32)
        _d = jax.random.randint(jax.random.fold_in(_gk, 3), (50000,), 0, 3125, jnp.int32)
        _loop = jnp.arange(3125, dtype=jnp.int32)
        src = jnp.concatenate([_s, _d, _loop])
        dst = jnp.concatenate([_d, _s, _loop])
        _o = jnp.argsort(dst, stable=True)
        src = src[_o]
        dst = dst[_o]
        edge_attr_16 = 0.000196303 + 1.00016 * jax.random.normal(jax.random.fold_in(_gk, 12), (103125, 16), jnp.float32)
        edge_attr_8 = -0.00010739 + 0.99994 * jax.random.normal(jax.random.fold_in(_gk, 13), (103125, 8), jnp.float32)
        edge_weight = jax.random.uniform(jax.random.fold_in(_gk, 15), (103125,), jnp.float32, 0.0, 1)
        return (x, src, dst, edge_attr_16, edge_attr_8, edge_weight)
    x, src, dst, edge_attr_16, edge_attr_8, edge_weight = _rec_inputs()

    def _L0_gnn_setup():
        import jax, jax.numpy as jnp
        import numpy as np
        N_NODES = 50000
        N_EDGES = 50000
        D = 64
        H = 8
        HD = D // H
        RAD_IN = 8
        SPH_IN = 16
        HIDDEN = 64
        AVG_NUM_NEIGHBORS = 32.0

        def _mlp2(x, W1, b1, W2, b2):
            return jax.nn.silu(x @ W1 + b1) @ W2 + b2
        key = jax.random.key(seed)
        ks = jax.random.split(key, 16)
        glorot = jax.nn.initializers.glorot_uniform()
        return {'node_feats': jax.random.normal(ks[0], (N_NODES, D), jnp.float32), 'edge_feats': jax.random.normal(ks[1], (N_EDGES, RAD_IN), jnp.float32), 'chi_scalar': jax.random.normal(ks[2], (N_EDGES, SPH_IN), jnp.float32), 'cutoffs': jax.random.uniform(ks[3], (N_EDGES,), jnp.float32), 'W_rad1': glorot(ks[4], (RAD_IN, HIDDEN), jnp.float32), 'b_rad1': jnp.zeros((HIDDEN,), jnp.float32), 'W_rad2': glorot(ks[5], (HIDDEN, H * HD), jnp.float32), 'b_rad2': jnp.zeros((H * HD,), jnp.float32), 'W_sph1': glorot(ks[6], (SPH_IN, HIDDEN), jnp.float32), 'b_sph1': jnp.zeros((HIDDEN,), jnp.float32), 'W_sph2': glorot(ks[7], (HIDDEN, H * HD), jnp.float32), 'b_sph2': jnp.zeros((H * HD,), jnp.float32), 'Wq': glorot(ks[8], (D, D), jnp.float32), 'Wk': glorot(ks[9], (D, D), jnp.float32), 'Wv': glorot(ks[10], (D, D), jnp.float32), 'senders': jax.random.randint(ks[11], (N_EDGES,), 0, N_NODES, jnp.int32), 'receivers': jax.random.randint(ks[12], (N_EDGES,), 0, N_NODES, jnp.int32)}
    _L0_gnn_all = _L0_gnn_setup()
    _L0_gnn_in = {k: v for k, v in _L0_gnn_all.items() if k in ('W_rad1', 'b_rad1', 'W_rad2', 'b_rad2', 'W_sph1', 'b_sph1', 'W_sph2', 'b_sph2', 'Wq', 'Wk', 'Wv')}
    del _L0_gnn_all

    def _L1_gnn_setup():
        import jax, jax.numpy as jnp
        import numpy as np
        N_NODES = 50000
        N_EDGES = 25000

        def gat_layer(x, src, dst, W, a_s, a_d, b, concat):
            N = x.shape[0]
            H, C = a_s.shape
            h = (x @ W).reshape(N, H, C)
            alpha_s = jnp.einsum('nhc,hc->nh', h, a_s)
            alpha_d = jnp.einsum('nhc,hc->nh', h, a_d)
            logits = jax.nn.leaky_relu(alpha_s[src] + alpha_d[dst], 0.2)
            m = jax.ops.segment_max(logits, dst, num_segments=N)
            e = jnp.exp(logits - m[dst])
            s = jax.ops.segment_sum(e, dst, num_segments=N)
            a = e / s[dst]
            out = jax.ops.segment_sum(h[src] * a[:, :, None], dst, num_segments=N)
            out = out.reshape(N, H * C) if concat else out.mean(axis=1)
            return out + b
        key = jax.random.key(seed)
        ks = jax.random.split(key, 10)
        in_c, hid, heads, out_c = (64, 64, 2, 64)
        x = jax.random.normal(ks[0], (N_NODES, in_c), dtype=jnp.float32)
        edge_index = jax.random.randint(ks[1], (2, N_EDGES), 0, N_NODES, dtype=jnp.int64)
        sc = lambda f: 1.0 / np.sqrt(f)
        W1 = jax.random.normal(ks[2], (in_c, heads * hid), dtype=jnp.float32) * sc(in_c)
        as1 = jax.random.normal(ks[3], (heads, hid), dtype=jnp.float32) * sc(hid)
        ad1 = jax.random.normal(ks[4], (heads, hid), dtype=jnp.float32) * sc(hid)
        b1 = jnp.zeros((heads * hid,), dtype=jnp.float32)
        W2 = jax.random.normal(ks[5], (heads * hid, heads * out_c), dtype=jnp.float32) * sc(heads * hid)
        as2 = jax.random.normal(ks[6], (heads, out_c), dtype=jnp.float32) * sc(out_c)
        ad2 = jax.random.normal(ks[7], (heads, out_c), dtype=jnp.float32) * sc(out_c)
        b2 = jnp.zeros((out_c,), dtype=jnp.float32)
        return {'x': x, 'edge_index': edge_index, 'W1': W1, 'as1': as1, 'ad1': ad1, 'b1': b1, 'W2': W2, 'as2': as2, 'ad2': ad2, 'b2': b2}
    _L1_gnn_all = _L1_gnn_setup()
    _L1_gnn_in = {k: v for k, v in _L1_gnn_all.items() if k in ('W1', 'as1', 'ad1', 'b1', 'W2', 'as2', 'ad2', 'b2')}
    del _L1_gnn_all
    return {'x': x, 'src': src, 'dst': dst, 'edge_attr_16': edge_attr_16, 'edge_attr_8': edge_attr_8, 'edge_weight': edge_weight, 'L0_gnn_W_rad1': _L0_gnn_in['W_rad1'], 'L0_gnn_b_rad1': _L0_gnn_in['b_rad1'], 'L0_gnn_W_rad2': _L0_gnn_in['W_rad2'], 'L0_gnn_b_rad2': _L0_gnn_in['b_rad2'], 'L0_gnn_W_sph1': _L0_gnn_in['W_sph1'], 'L0_gnn_b_sph1': _L0_gnn_in['b_sph1'], 'L0_gnn_W_sph2': _L0_gnn_in['W_sph2'], 'L0_gnn_b_sph2': _L0_gnn_in['b_sph2'], 'L0_gnn_Wq': _L0_gnn_in['Wq'], 'L0_gnn_Wk': _L0_gnn_in['Wk'], 'L0_gnn_Wv': _L0_gnn_in['Wv'], 'L1_gnn_W1': _L1_gnn_in['W1'], 'L1_gnn_as1': _L1_gnn_in['as1'], 'L1_gnn_ad1': _L1_gnn_in['ad1'], 'L1_gnn_b1': _L1_gnn_in['b1'], 'L1_gnn_W2': _L1_gnn_in['W2'], 'L1_gnn_as2': _L1_gnn_in['as2'], 'L1_gnn_ad2': _L1_gnn_in['ad2'], 'L1_gnn_b2': _L1_gnn_in['b2']}

def reference(x, src, dst, edge_attr_16, edge_attr_8, edge_weight, L0_gnn_W_rad1, L0_gnn_b_rad1, L0_gnn_W_rad2, L0_gnn_b_rad2, L0_gnn_W_sph1, L0_gnn_b_sph1, L0_gnn_W_sph2, L0_gnn_b_sph2, L0_gnn_Wq, L0_gnn_Wk, L0_gnn_Wv, L1_gnn_W1, L1_gnn_as1, L1_gnn_ad1, L1_gnn_b1, L1_gnn_W2, L1_gnn_as2, L1_gnn_ad2, L1_gnn_b2):
    import jax
    import jax.numpy as jnp

    def _L0_gnn_ref(node_feats, edge_feats, chi_scalar, cutoffs, W_rad1, b_rad1, W_rad2, b_rad2, W_sph1, b_sph1, W_sph2, b_sph2, Wq, Wk, Wv, senders, receivers):
        import jax, jax.numpy as jnp
        import numpy as np
        N_NODES = 50000
        N_EDGES = 50000
        D = 64
        H = 8
        HD = D // H
        RAD_IN = 8
        SPH_IN = 16
        HIDDEN = 64
        AVG_NUM_NEIGHBORS = 32.0

        def _mlp2(x, W1, b1, W2, b2):
            return jax.nn.silu(x @ W1 + b1) @ W2 + b2
        w_ij = _mlp2(edge_feats, W_rad1, b_rad1, W_rad2, b_rad2)
        w_ij = w_ij + _mlp2(chi_scalar, W_sph1, b_sph1, W_sph2, b_sph2)
        w_ij = w_ij.reshape(-1, H, HD)
        q_i = (node_feats @ Wq).reshape(-1, H, HD)[receivers]
        k_j = (node_feats @ Wk).reshape(-1, H, HD)[senders]
        alpha = (q_i * w_ij * k_j).sum(axis=-1) / jnp.sqrt(jnp.float32(HD))
        alpha = alpha * cutoffs[:, None]
        v_j = (node_feats @ Wv)[senders].reshape(-1, H, HD)
        out = jax.ops.segment_sum(alpha[..., None] * v_j, receivers, num_segments=node_feats.shape[0]) / AVG_NUM_NEIGHBORS
        return out.reshape(-1, H * HD)

    def _L1_gnn_ref(x, edge_index, W1, as1, ad1, b1, W2, as2, ad2, b2):
        import jax, jax.numpy as jnp
        import numpy as np
        N_NODES = 50000
        N_EDGES = 25000

        def gat_layer(x, src, dst, W, a_s, a_d, b, concat):
            N = x.shape[0]
            H, C = a_s.shape
            h = (x @ W).reshape(N, H, C)
            alpha_s = jnp.einsum('nhc,hc->nh', h, a_s)
            alpha_d = jnp.einsum('nhc,hc->nh', h, a_d)
            logits = jax.nn.leaky_relu(alpha_s[src] + alpha_d[dst], 0.2)
            m = jax.ops.segment_max(logits, dst, num_segments=N)
            e = jnp.exp(logits - m[dst])
            s = jax.ops.segment_sum(e, dst, num_segments=N)
            a = e / s[dst]
            out = jax.ops.segment_sum(h[src] * a[:, :, None], dst, num_segments=N)
            out = out.reshape(N, H * C) if concat else out.mean(axis=1)
            return out + b
        N = x.shape[0]
        loops = jnp.arange(N, dtype=edge_index.dtype)
        src = jnp.concatenate([edge_index[0], loops])
        dst = jnp.concatenate([edge_index[1], loops])
        h = gat_layer(x, src, dst, W1, as1, ad1, b1, concat=True)
        out = gat_layer(h, src, dst, W2, as2, ad2, b2, concat=False)
        return out
    edge_index = jnp.stack([src, dst])
    x = _layernorm(x + _L0_gnn_ref(x, edge_attr_8, edge_attr_16, edge_weight, L0_gnn_W_rad1, L0_gnn_b_rad1, L0_gnn_W_rad2, L0_gnn_b_rad2, L0_gnn_W_sph1, L0_gnn_b_sph1, L0_gnn_W_sph2, L0_gnn_b_sph2, L0_gnn_Wq, L0_gnn_Wk, L0_gnn_Wv, src, dst), axis=-1)
    x = _layernorm(x + _L1_gnn_ref(x, edge_index, L1_gnn_W1, L1_gnn_as1, L1_gnn_ad1, L1_gnn_b1, L1_gnn_W2, L1_gnn_as2, L1_gnn_ad2, L1_gnn_b2), axis=-1)
    return x

_drawn_inputs = setup_inputs


def setup_inputs(seed=0):
    import zlib

    import numpy as np

    out = dict(_drawn_inputs(seed))
    spreads = {'L0_gnn_b_rad1': (0.0, 0.8),
     'L0_gnn_b_rad2': (0.0, 0.772),
     'L0_gnn_b_sph1': (0.0, 0.8),
     'L0_gnn_b_sph2': (0.0, 0.619),
     'L1_gnn_b1': (0.0, 0.1),
     'L1_gnn_b2': (0.0, 0.1)}
    factors = {'L1_gnn_ad1': 54.702, 'L1_gnn_as2': 4.33, 'L1_gnn_ad2': 83.018}
    for name, (base, spread) in spreads.items():
        noise = np.random.default_rng([zlib.crc32(name.encode()), seed]).standard_normal(out[name].shape)
        drawn = base * np.exp(spread * noise) if base else spread * noise
        out[name] = jnp.asarray(drawn.astype(out[name].dtype))
    for name, factor in factors.items():
        out[name] = (out[name] * factor).astype(out[name].dtype)
    return out
```

```python
import concourse.bass as bass
from concourse import mybir
from concourse.alu_op_type import AluOpType as ALU
from contextlib import ExitStack

P = 128
N, D, E = 3125, 64, 103125
NT = -(-N // P)
TAIL = N - (NT - 1) * P
NCH = -(-E // P)
G = 4
STEPS = 4
BODY = G * STEPS
NI = -(-(NCH + NT - 1) // BODY) * BODY
NB = NI // BODY
KB = -(-NI // P)
NIP = KB * P
NG = NI // G
RING = NI // 13
RG = RING // G
HALF = RING // 2
F8, F16 = 8, 16
F = F8 + F16
EP = NIP * P
DST_PAD = 4095
HEADS, HD = 8, 8
NX = 5
H, C = 2, 64
AVG = 32.0
EPS = 1e-5
BIG = 2.0 ** 100
BANK = 512
TG = 5


def gnn(nc, x, src_rows, dst_rows, ew_rows, attrs, w_rad1, b_rad1, w_rad2, b_rad2, w_sph1, b_sph1, w_sph2, b_sph2,
        wq, wk, wv, g1_w, g1_as, g1_ad, g1_b, g2_w, g2_as, g2_ad, g2_b, out):
    f32, bf16, i32 = mybir.dt.float32, mybir.dt.bfloat16, mybir.dt.int32
    ACT = mybir.ActivationFunctionType
    AX = mybir.AxisListType
    ET = mybir.EngineType
    ds = bass.ds
    ctx = ExitStack()
    with ctx:
        def sb(name, shape, dt=f32):
            return ctx.enter_context(nc.sbuf_tensor(name, shape, dt))

        def sem(name):
            return ctx.enter_context(nc.semaphore(name))

        table = nc.dram_tensor("table", [NT * P, P], f32, kind="Internal").ap()
        dl_dram = nc.dram_tensor("dl_dram", [NIP * P], bf16, kind="Internal").ap()
        sl_dram = nc.dram_tensor("sl_dram", [NIP * P], bf16, kind="Internal").ap()

        iota_f = sb("iota_f", [P, P])
        iota_p = sb("iota_p", [P, 1])
        iota_t = sb("iota_t", [P, NT])
        tile_no = sb("tile_no", [P, NT - 1])
        item_no = sb("item_no", [P, KB])
        ident = sb("ident", [P, P])
        ones = sb("ones", [P, P])
        ones_bf = sb("ones_bf", [1, P], bf16)
        zeros_bf = sb("zeros_bf", [1, BANK], bf16)
        w_in = sb("w_in", [F, P])
        b_in = sb("b_in", [P, 1])
        w_out = sb("w_out", [P, D])
        b_out2 = sb("b_out2", [1, 2, D])
        b_out = sb("b_out", [1, G, D])
        w_qkv = sb("w_qkv", [D, 3 * D])
        w1x = sb("w1x", [D, H * C + 4])
        w2x = sb("w2x", [P, H * C + 4])
        att = sb("att", [P, 4, H * C])
        att_prod = sb("att_prod", [P, H * C])
        b1_b = sb("b1_b", [P, H * C])
        b2_b = sb("b2_b", [P, C])
        x1 = sb("x1", [P, NT * D])
        h_in = sb("h_in", [P, NT * H * C])
        stat = sb("stat", [P, 4, NT])
        node_m = sb("node_m", [P, 6, NT * H])
        part3 = h_in[:, 0:3 * NT * D // 2].bitcast(bf16).rearrange("p (s n) -> p s n", s=3)
        asd = sb("asd", [P, NT, 4])
        res = sb("res", [P, 2, NT * 4])
        as3 = sb("as3", [P, 3, H, NT], bf16)
        ad3 = sb("ad3", [P, 3, NT * H], bf16)
        stage = sb("stage", [P, TG * P])
        xT = sb("xT", [P, TG * P])
        last_i = sb("last_i", [P, KB], i32)
        last_f = sb("last_f", [P, KB])
        cmp_a = sb("cmp_a", [P, KB * (NT - 1)])
        cnt = sb("cnt", [P, NT - 1])
        first_item = sb("first_item", [P, NT - 1])
        t_col = sb("t_col", [P, KB])
        t128 = sb("t128", [P, KB])
        c_col = sb("c_col", [P, KB])
        c_idx = sb("c_idx", [P, KB], i32)
        t_row = sb("t_row", [1, NIP], i32)
        c_row = sb("c_row", [1, NIP], i32)
        tmp_r = sb("tmp_r", [P, KB, P])
        src_e = sb("src_e", [P, NIP], i32)
        idx = sb("idx", [P, RING], i32)
        dl_e = sb("dl_e", [P, NIP])
        hi_e = sb("hi_e", [P, NIP])
        ew_e = sb("ew_e", [P, NIP])
        keep_f = sb("keep_f", [P, KB, P], bf16)
        keep_b = sb("keep_b", [P, KB, P], bf16)
        not_first = sb("not_first", [P, KB, P], bf16)
        not_last = sb("not_last", [P, KB, P], bf16)
        ends = sb("ends", [1, 2, NIP])
        links = sb("links", [1, 4, NIP], bf16)
        runs = sb("runs", [1, 2, NIP])
        carry_c = sb("carry_c", [P, 2 * KB])
        edge_x = sb("edge_x", [P, (H + NX) * NIP])
        l_r = edge_x[:, 0:H * NIP].rearrange("p (h n) -> p h n", h=H)
        ex = edge_x[:, H * NIP:(H + NX) * NIP].rearrange("p (q n) -> p q n", q=NX)
        p_e, l_e, ind_e = ex[:, 0:H, :], ex[:, H:2 * H, :], ex[:, 2 * H, :]
        t_a = edge_x[:, 2 * H * NIP:2 * H * NIP + NT * D]
        kv_rows = edge_x[:, 0:NT * P].rearrange("p (t f) -> p t f", f=P)
        ring = sb("ring", [P, RING, P])
        attrs_t = sb("attrs_t", [F, 2, G * P])
        hid_s = sb("hid_s", [P, 2, G * P])
        bc_d = sb("bc_d", [P, 2, 8 * P], bf16)
        bc_s = sb("bc_s", [P, 2, 8 * P], bf16)
        oh_n = sb("oh_n", [P, 4, G * P], bf16)
        work = sb("work", [P, 2 * STEPS, G * P])
        oh_e, msg = work[:, 0:STEPS, :], work[:, STEPS:2 * STEPS, :]
        blk = lambda n: work[:, 2 * n:2 * n + 2, :].rearrange("p a n -> p (a n)")[:, 0:KB * P].rearrange("p (k e) -> p k e", e=P)
        src_r, dst_ri, ew_r, tmp_i = blk(0).bitcast(i32), blk(1).bitcast(i32), blk(2), blk(3).bitcast(i32)
        bf_r = [bc_s[:, n, 0:KB * P] for n in range(2)]
        dst_r = sb("dst_r", [P, KB, P])
        oh_hi = sb("oh_hi", [P, 2, 8 * NT])
        t1 = sb("t1", [P, G * D])
        t2 = sb("t2", [P, G * D])
        sel = sb("sel", [P, 8 * H * NT])
        al = sb("al", [P, G * HEADS])
        alw = sb("alw", [P, G * HEADS])
        as_g = sb("as_g", [P, 8 * H])

        h_rows = h_in[:].rearrange("p (t f) -> p t f", f=P)

        ps = ctx.enter_context(nc.psum_tensor("ps", [P, 8 * BANK], f32))
        HID = 4 * BANK
        WQ = 6 * BANK
        SUMS = 6 * BANK + NT * H * C - 6 * BANK
        assert SUMS + NT * NX <= 7 * BANK

        consts_made = sem("consts_made")
        consts_f = sem("consts_f")
        weights_in = sem("weights_in")
        x_in = sem("x_in")
        last_in = sem("last_in")
        cnt_ready = sem("cnt_ready")
        cs_ready = sem("cs_ready")
        cidx_ready = sem("cidx_ready")
        tc_ready = sem("tc_ready")
        tcrow_mm = sem("tcrow_mm")
        rows_t = sem("rows_t")
        rows_gathered = sem("rows_gathered")
        bfrow_ready = sem("bfrow_ready")
        bfrow_out = sem("bfrow_out")
        tr_ready = sem("tr_ready")
        tr_mm = sem("tr_mm")
        tr_done = sem("tr_done")
        items_ready = sem("items_ready")
        chain = sem("chain")
        achain = sem("achain")
        zeroed = sem("zeroed")
        in_ready = sem("in_ready")
        stage_ready = sem("stage_ready")
        stage_mm = sem("stage_mm")
        xT_ready = sem("xT_ready")
        proj_mm = sem("proj_mm")
        proj_free = sem("proj_free")
        rows_ready = sem("rows_ready")
        rows_written = sem("rows_written")
        proj_done = sem("proj_done")
        parts_ready = sem("parts_ready")
        idx_staged = sem("idx_staged")
        g_sem = [sem(f"g_sem{i}") for i in range(4)]
        gathered = sem("gathered")
        ring_free = sem("ring_free")
        at_ready = [sem(f"at_ready{i}") for i in range(2)]
        at_free = sem("at_free")
        bd_ready = [sem(f"bd_ready{i}") for i in range(2)]
        bd_free = sem("bd_free")
        hid_mm = sem("hid_mm")
        hs_ready = sem("hs_ready")
        hs_free = sem("hs_free")
        ohn_ready = sem("ohn_ready")
        wq_ready = sem("wq_ready")
        wq_free = sem("wq_free")
        msg_ready = sem("msg_ready")
        oh_free = sem("oh_free")
        sel_oh = sem("sel_oh")
        sel_mm = sem("sel_mm")
        sel_free = sem("sel_free")
        lrow_ready = sem("lrow_ready")
        lrow_mm = sem("lrow_mm")
        ends_ready = sem("ends_ready")
        ends_mm = sem("ends_mm")
        carry_ready = sem("carry_ready")
        carry_mm = sem("carry_mm")
        shift_ready = sem("shift_ready")
        exp_ready = sem("exp_ready")
        prow_mm = sem("prow_mm")
        exp_nodes = sem("exp_nodes")
        p_ready = sem("p_ready")
        acc_free = sem("acc_free")
        var_ready = sem("var_ready")
        sd_ready = sem("sd_ready")
        out_ready = sem("out_ready")
        out_done = sem("out_done")

        def load_regs(engine, row, at, n, top):
            _, v = nc.values_load_multi_w_load_instructions(
                row[0:1, ds(at, n)], engines=[engine], min_val=0, max_val=top,
                skip_runtime_bounds_check_because="worked out as a count of at most that many")
            return v

        block = ctx.enter_context(nc.Block())

        @block.sync
        def _(sp):
            sp.dma_start(last_i[:], dst_rows.rearrange("(k p) e -> p k e", p=P)[:, :, P - 1],
                         allow_slow_non_contiguous=True).then_inc(last_in, 16)
            sp.dma_start(x1[:, 0:(NT - 1) * D].rearrange("p (t d) -> p t d", d=D),
                         x[0:(NT - 1) * P, :].rearrange("(t p) d -> p t d", p=P)).then_inc(x_in, 16)
            sp.wait_ge(consts_f, 1)
            sp.dma_start(x1[0:TAIL, (NT - 1) * D:NT * D], x[(NT - 1) * P:N, :]).then_inc(x_in, 16)
            n = 0
            for dst, s in ((w_in[0:F8, 0:D], w_rad1), (w_in[F8:F, D:2 * D], w_sph1),
                           (b_in[0:D, :], b_rad1.rearrange("(d a) -> d a", a=1)),
                           (b_in[D:P, :], b_sph1.rearrange("(d a) -> d a", a=1)),
                           (w_out[0:D, :], w_rad2), (w_out[D:P, :], w_sph2),
                           (b_out2[0:1, 0, :], b_rad2.rearrange("(a d) -> a d", a=1)),
                           (b_out2[0:1, 1, :], b_sph2.rearrange("(a d) -> a d", a=1)),
                           (w_qkv[:, 0:D], wq), (w_qkv[:, D:2 * D], wk), (w_qkv[:, 2 * D:3 * D], wv),
                           (w1x[:, 0:H * C], g1_w), (w2x[:, 0:H * C], g2_w),
                           (att[:, 0, :], g1_as.rearrange("h c -> (h c)").partition_broadcast(P)),
                           (att[:, 1, :], g1_ad.rearrange("h c -> (h c)").partition_broadcast(P)),
                           (att[:, 2, :], g2_as.rearrange("h c -> (h c)").partition_broadcast(P)),
                           (att[:, 3, :], g2_ad.rearrange("h c -> (h c)").partition_broadcast(P)),
                           (b1_b[:], g1_b.partition_broadcast(P)), (b2_b[:], g2_b.partition_broadcast(P))):
                sp.dma_start(dst, s).then_inc(weights_in, 16)
                n += 1
            assert n == N_WEIGHTS
            sp.wait_ge(bfrow_ready, 1)
            sp.sem_inc(bfrow_ready, -1)
            sp.dma_start(dl_dram.rearrange("(k p e) -> p k e", p=P, e=P),
                         bf_r[0].rearrange("p (k e) -> p k e", e=P)).then_inc(bfrow_out, 16)
            sp.dma_start(sl_dram.rearrange("(k p e) -> p k e", p=P, e=P),
                         bf_r[1].rearrange("p (k e) -> p k e", e=P)).then_inc(bfrow_out, 16)

            def write_table(row_out):
                with sp.Fori(0, NT // TG) as i:
                    sp.wait_ge(rows_ready, 1)
                    sp.sem_inc(rows_ready, -1)
                    sp.dma_start(table.rearrange("(t p) f -> p t f", p=P)[:, ds(i * TG, TG), :],
                                 row_out[:, ds(i * TG, TG), :]).then_inc(rows_written, 16)

            write_table(kv_rows)
            sp.wait_ge(bfrow_out, 32)
            sp.wait_ge(items_ready, 1)
            sp.sem_inc(items_ready, -1)
            with sp.Fori(0, NB) as it:
                for hb in range(2):
                    sp.wait_ge(bd_free, 1)
                    sp.sem_inc(bd_free, -1)
                    sp.dma_start(bc_d[:, hb, :], dl_dram[ds(it * (BODY * P) + hb * 8 * P, 8 * P)].partition_broadcast(P)
                                 ).then_inc(bd_ready[hb], 16)
                    cs = load_regs(ET.SP, c_row, it * BODY + hb * 8, 8, NIP - 1)
                    for gb in range(2):
                        sp.wait_ge(at_free, 1)
                        sp.sem_inc(at_free, -1)
                        for j in range(G):
                            sp.dma_start(attrs_t[:, gb, j * P:(j + 1) * P], attrs[:, ds(cs[gb * G + j] * P, P)]
                                         ).then_inc(at_ready[gb], 16)
            for layer in range(2):
                write_table(h_rows)
                with sp.Fori(0, NB) as it:
                    for hb in range(2):
                        sp.wait_ge(bd_free, 1)
                        sp.sem_inc(bd_free, -1)
                        at = it * (BODY * P) + hb * 8 * P
                        sp.dma_start(bc_d[:, hb, :], dl_dram[ds(at, 8 * P)].partition_broadcast(P)
                                     ).then_inc(bd_ready[hb], 16)
                        sp.dma_start(bc_s[:, hb, :], sl_dram[ds(at, 8 * P)].partition_broadcast(P)
                                     ).then_inc(bd_ready[hb], 16)
            sp.wait_ge(out_ready, 1)
            sp.sem_inc(out_ready, -1)
            sp.dma_start(out[0:(NT - 1) * P, :].rearrange("(t p) d -> p t d", p=P),
                         t_a[:, 0:(NT - 1) * D].rearrange("p (t d) -> p t d", d=D)).then_inc(out_done, 16)
            sp.dma_start(out[(NT - 1) * P:N, :], t_a[0:TAIL, (NT - 1) * D:NT * D]).then_inc(out_done, 16)
            sp.wait_ge(out_done, 32)

        @block.gpsimd
        def _(pool):
            g = nc.gpsimd
            g.iota(iota_f[:], [[1, P]], base=0, channel_multiplier=0, allow_small_or_imprecise_dtypes=True)
            g.iota(iota_p[:], [[1, 1]], base=0, channel_multiplier=1, allow_small_or_imprecise_dtypes=True)
            g.iota(iota_t[:], [[1, NT]], base=0, channel_multiplier=0, allow_small_or_imprecise_dtypes=True)
            g.iota(tile_no[:], [[1, NT - 1]], base=1, channel_multiplier=0, allow_small_or_imprecise_dtypes=True)
            g.iota(item_no[:], [[P, KB]], base=0, channel_multiplier=1,
                   allow_small_or_imprecise_dtypes=True).then_inc(consts_made, 1)
            pool.wait_ge(cidx_ready, 1)
            pool.sem_inc(cidx_ready, -1)
            for k in range(KB):
                for dst, rows in ((dst_ri, dst_rows), (src_r, src_rows), (ew_r, ew_rows)):
                    g.indirect_dma_start(dst[:, k, :], None, rows, bass.IndirectOffsetOnAxis(c_idx[:, k:k + 1], 0)
                                         ).then_inc(rows_gathered, 16)
            pool.sem_inc(ring_free, RG)
            pool.wait_ge(rows_t, 1)

            def pass_on(layer, turn, q):
                turns = layer * (NI // RING) + turn
                pool.wait_ge(g_sem[q % 4], turns * (16 * G * RG // 4) + 16 * G * (q // 4 + 1))
                pool.sem_inc(gathered, 1)

            with pool.Fori(0, 3) as layer:
                pool.wait_ge(rows_written, 16 * (NT // TG))
                pool.sem_inc(rows_written, -(16 * (NT // TG)))
                with pool.Fori(0, NI // RING) as turn:
                    for q in range(RG):
                        if q % (RG // 2) == 0:
                            s0 = q * G
                            g.tensor_copy(idx[:, s0:s0 + HALF], src_e[:, ds(turn * RING + s0, HALF)]
                                          ).then_inc(idx_staged, 1)
                            pool.wait_ge(idx_staged, 1)
                            pool.sem_inc(idx_staged, -1)
                        pool.wait_ge(ring_free, 1)
                        pool.sem_inc(ring_free, -1)
                        for j in range(G):
                            s = q * G + j
                            g.indirect_dma_start(ring[:, s, :], None, table,
                                                 bass.IndirectOffsetOnAxis(idx[:, s:s + 1], 0)
                                                 ).then_inc(g_sem[q % 4], 16)
                        if q >= 3:
                            pass_on(layer, turn, q - 3)
                    for q in range(RG - 3, RG):
                        pass_on(layer, turn, q)

        @block.scalar
        def _(act):
            a = nc.scalar

            def evacuate(width, row_out, first, n_side, side):
                with act.Fori(0, NT // TG) as i:
                    act.wait_ge(stage_mm, 1)
                    act.sem_inc(stage_mm, -1)
                    a.copy(xT[0:width, :], ps[0:width, 0:TG * P]).then_inc(xT_ready, 1)
                    act.wait_ge(proj_mm, 1)
                    act.sem_inc(proj_mm, -1)
                    pr = ps[:, 2 * BANK:2 * BANK + TG * 256].rearrange("p (t f) -> p t f", f=256)
                    a.copy(row_out[:, ds(i * TG, TG), :], pr[:, :, first:first + P]).then_inc(rows_ready, 1)
                    o = 0 if first else P
                    a.copy(side[:, ds(i * TG * n_side, TG * n_side)].rearrange("p (t f) -> p t f", f=n_side),
                           pr[:, :, o:o + n_side]).then_inc(proj_free, 1)
                act.drain().then_inc(proj_done, 1)

            def sqrt_var():
                act.wait_ge(var_ready, 1)
                act.sem_inc(var_ready, -1)
                a.activation(stat[:, 2, :], stat[:, 1, :], ACT.Sqrt).then_inc(sd_ready, 1)

            evacuate(D, kv_rows, D, D, t_a)

            def silu(gb):
                act.wait_ge(hid_mm, 1)
                act.sem_inc(hid_mm, -1)
                act.sem_inc(at_free, 1)
                act.wait_ge(hs_free, 1)
                act.sem_inc(hs_free, -1)
                a.activation(hid_s[:, gb, :], ps[:, HID + gb * BANK:HID + (gb + 1) * BANK], ACT.Silu,
                             bias=b_in[:, 0:1]).then_inc(hs_ready, 1)

            act.wait_ge(weights_in, 16 * N_WEIGHTS)
            act.sem_inc(at_free, 2)
            with act.Fori(0, NG // 2) as it:
                silu(0)
                silu(1)
            sqrt_var()
            for layer in range(2):
                evacuate(D if layer == 0 else P, h_rows, 0, 4, asd[:, :, :].rearrange("p t f -> p (t f)"))
                for h in range(H):
                    act.wait_ge(shift_ready, 1)
                    act.sem_inc(shift_ready, -1)
                    a.activation(l_r[:, h, :], l_r[:, h, :], ACT.Exp).then_inc(exp_ready, 1)
                act.wait_ge(shift_ready, 1)
                act.sem_inc(shift_ready, -1)
                a.activation(node_m[:, 4:6, :], node_m[:, 2:4, :], ACT.Exp).then_inc(exp_nodes, 1)
            sqrt_var()

        @block.vector
        def _(dve):
            v = nc.vector

            def link(ins, n=1):
                ins.then_inc(chain, 1)
                dve.wait_ge(chain, 1)
                dve.sem_inc(chain, -1)

            v.memset(x1[:, (NT - 1) * D:NT * D], 0.0)
            v.memset(w_in[:], 0.0)
            v.memset(ones[:], 1.0)
            v.memset(ones_bf[:], 1.0)
            v.memset(zeros_bf[:], 0.0)
            v.memset(links[:], -BIG)
            v.memset(keep_f[:], -BIG)
            v.memset(keep_b[:], -BIG).then_inc(consts_f, 1)
            dve.wait_ge(consts_f, 1)
            dve.wait_ge(consts_made, 1)
            link(v.tensor_scalar(ident[:], iota_f[:], iota_p[:, 0:1], None, ALU.is_equal))
            dve.wait_ge(last_in, 16)
            link(v.tensor_copy(last_f[:], last_i[:]))
            ca = cmp_a[:].rearrange("p (t k) -> p t k", k=KB)
            link(v.tensor_scalar(cnt[:], tile_no[:], float(P), None, ALU.mult))
            link(v.tensor_tensor(ca, last_f[:].unsqueeze(1).to_broadcast([P, NT - 1, KB]),
                                 cnt[:].unsqueeze(2).to_broadcast([P, NT - 1, KB]), ALU.is_lt))
            v.tensor_reduce(cnt[:], ca, AX.X, ALU.add).then_inc(cnt_ready, 1)
            dve.wait_ge(cs_ready, 1)
            dve.sem_inc(cs_ready, -1)
            link(v.tensor_tensor(first_item[:], ps[:, 0:NT - 1], tile_no[:], ALU.add))
            cb = cmp_a[:].rearrange("p (k t) -> p k t", k=KB)
            link(v.tensor_tensor(cb, first_item[:].unsqueeze(1).to_broadcast([P, KB, NT - 1]),
                                 item_no[:].unsqueeze(2).to_broadcast([P, KB, NT - 1]), ALU.is_le))
            link(v.tensor_reduce(t_col[:], cb, AX.X, ALU.add))
            link(v.tensor_tensor(c_col[:], item_no[:], t_col[:], ALU.subtract))
            v.tensor_copy(c_idx[:], c_col[:]).then_inc(cidx_ready, 1)
            v.tensor_scalar(t128[:], t_col[:], float(P), None, ALU.mult).then_inc(tc_ready, 1)
            dve.wait_ge(tcrow_mm, 1)
            dve.sem_inc(tcrow_mm, -1)
            v.tensor_copy(t_row[:], ps[0:1, 0:NIP])
            v.tensor_copy(c_row[:], ps[0:1, 2 * BANK:2 * BANK + NIP]).then_inc(tr_done, 1)
            dve.wait_ge(weights_in, 16 * N_WEIGHTS)
            link(v.tensor_tensor(b_out[:, 0, :], b_out2[:, 0, :], b_out2[:, 1, :], ALU.add))
            v.tensor_copy(b_out[:, 1:G, :], b_out[:, 0:1, :].to_broadcast([1, G - 1, D]))
            for wx, np_, first in ((w1x, D, 0), (w2x, P, 2)):
                for s in range(2):
                    link(v.tensor_tensor(att_prod[0:np_, :], wx[:, 0:H * C], att[0:np_, first + s, :], ALU.mult))
                    link(v.tensor_reduce(wx[:, H * C + 2 * s:H * C + 2 * s + 2],
                                         att_prod[0:np_, :].rearrange("p (h c) -> p h c", c=C), AX.X, ALU.add))

            def stage_tiles(inp, width):
                with dve.Fori(0, NT // TG) as i:
                    dve.wait_ge(in_ready, 1)
                    dve.sem_inc(in_ready, -1)
                    v.tensor_copy(stage[:, 0:TG * width], inp[:, ds(i * TG * width, TG * width)]
                                  ).then_inc(stage_ready, 1)

            dve.wait_ge(x_in, 32)
            dve.sem_inc(in_ready, 1)
            stage_tiles(x1, D)
            dve.wait_ge(proj_done, 1)
            dve.sem_inc(proj_done, -1)

            def split3(srcv, dst3, r0, r1):
                link(v.tensor_copy(dst3[0], srcv))
                link(v.tensor_tensor(r0, srcv, dst3[0], ALU.subtract))
                link(v.tensor_copy(dst3[1], r0))
                link(v.tensor_tensor(r1, r0, dst3[1], ALU.subtract))
                return v.tensor_copy(dst3[2], r1)

            hf = NT * D // 2
            for a0 in (0, hf):
                link(split3(t_a[:, a0:a0 + hf], [part3[:, s, a0:a0 + hf] for s in range(3)],
                            h_in[:, 3 * hf:4 * hf], tmp_r[:].rearrange("p k e -> p (k e)")[:, 0:hf]))

            dve.wait_ge(rows_gathered, 16 * 3 * KB)
            link(v.tensor_copy(dst_r[:], dst_ri[:]))
            for k in range(KB):
                last = v.tensor_scalar(tmp_r[:, k, :], dst_r[:, k, :], t128[:, k:k + 1], None, ALU.subtract)
            link(last)
            v.tensor_scalar(bf_r[0], tmp_r[:].rearrange("p k e -> p (k e)"), -1.0, float(P), ALU.max, ALU.min)
            link(v.tensor_scalar(tmp_i[:], src_r[:], P - 1, None, ALU.bitwise_and))
            v.tensor_copy(bf_r[1], tmp_i[:].rearrange("p k e -> p (k e)")).then_inc(bfrow_ready, 1)

            def to_edges(dst):
                dve.sem_inc(tr_ready, 1)
                dve.wait_ge(tr_mm, 1)
                dve.sem_inc(tr_mm, -1)
                return v.tensor_copy(dst, ps[:, 2 * BANK:2 * BANK + NIP])

            link(to_edges(dl_e[:]))
            link(v.tensor_copy(tmp_r[:], src_r[:]))
            to_edges(src_e[:]).then_inc(rows_t, 1)
            link(v.tensor_scalar(tmp_i[:], src_r[:], 7, None, ALU.logical_shift_right))
            link(v.tensor_copy(tmp_r[:], tmp_i[:]))
            link(to_edges(hi_e[:]))
            link(v.tensor_scalar(tmp_r[:], ew_r[:], 1.0 / (AVG * HD ** 0.5), None, ALU.mult))
            link(to_edges(ew_e[:]))

            def mask(dst, a_, b_):
                link(v.tensor_tensor(dst, a_, b_, ALU.not_equal))
                link(v.tensor_scalar(dst, dst, -BIG, None, ALU.mult))

            mask(keep_f[:, :, 1:P], dst_r[:, :, 1:P], dst_r[:, :, 0:P - 1])
            mask(keep_b[:, :, 0:P - 1], dst_r[:, :, 1:P], dst_r[:, :, 0:P - 1])
            for k in range(KB):
                v.tensor_scalar(not_first[:, k, :], dst_r[:, k, :], dst_r[:, k, 0:1], -BIG, ALU.not_equal, ALU.mult)
                last = v.tensor_scalar(not_last[:, k, :], dst_r[:, k, :], dst_r[:, k, P - 1:P], -BIG,
                                       ALU.not_equal, ALU.mult)
            link(last)

            def to_rows(dst, a_, b_):
                v.tensor_copy(carry_c[:, 0:KB], a_)
                v.tensor_copy(carry_c[:, KB:2 * KB], b_).then_inc(ends_ready, 1)
                dve.wait_ge(ends_mm, 1)
                dve.sem_inc(ends_mm, -1)
                v.tensor_copy(dst[:, 0, :], ps[0:1, 0:NIP])
                return v.tensor_copy(dst[:, 1, :], ps[0:1, 2 * BANK:2 * BANK + NIP])

            link(to_rows(ends, dst_r[:, :, 0], dst_r[:, :, P - 1]))
            carry = ends
            e0, e1 = ends[:, 0, :], ends[:, 1, :]
            R = NIP
            link(v.tensor_tensor(runs[:, 1, 0:R - 1], t_row[:, 1:R], t_row[:, 0:R - 1], ALU.not_equal))

            def link_mask(dst, a_, b_):
                link(v.tensor_tensor(runs[:, 0, 0:R - 1], a_, b_, ALU.not_equal))
                link(v.tensor_tensor(runs[:, 0, 0:R - 1], runs[:, 0, 0:R - 1], runs[:, 1, 0:R - 1], ALU.max))
                link(v.tensor_scalar(dst, runs[:, 0, 0:R - 1], -BIG, None, ALU.mult))

            link_mask(links[:, 0, 1:R], e1[:, 0:R - 1], e1[:, 1:R])
            link_mask(links[:, 1, 0:R - 1], e0[:, 1:R], e0[:, 0:R - 1])
            link_mask(links[:, 2, 1:R], e1[:, 0:R - 1], e0[:, 1:R])
            link_mask(links[:, 3, 0:R - 1], e0[:, 1:R], e1[:, 0:R - 1])
            v.memset(ends[:, :, R - 1:R], 1.0)
            v.tensor_copy(ends[:, 0, 0:R - 1], runs[:, 0, 0:R - 1]).then_inc(carry_ready, 1)
            dve.wait_ge(carry_mm, 1)
            dve.sem_inc(carry_mm, -1)
            link(v.tensor_tensor(tmp_r[:, :, 0:P - 1], dst_r[:, :, 1:P], dst_r[:, :, 0:P - 1], ALU.not_equal))
            link(v.tensor_copy(tmp_r[:, :, P - 1], ps[:, 0:KB]))
            link(to_edges(ind_e))
            dve.sem_inc(parts_ready, 1)

            def one_hot_nodes(o, hb, half):
                return v.tensor_scalar(oh_n[:, o, :], bc_d[:, hb, half * G * P:(half + 1) * G * P], iota_p[:, 0:1],
                                       None, ALU.is_equal)

            def make0(it, j):
                dve.wait_ge(oh_free, 1)
                dve.sem_inc(oh_free, -1)
                if j % 2 == 0:
                    dve.wait_ge(bd_ready[j // 2], 16)
                    dve.sem_inc(bd_ready[j // 2], -16)
                one_hot_nodes(j, j // 2, j % 2).then_inc(ohn_ready, 1)
                for i in range(G):
                    v.tensor_scalar(oh_e[:, j, i * P:(i + 1) * P], iota_f[:], dl_e[:, ds(it * BODY + j * G + i, 1)],
                                    None, ALU.is_equal)

            def edges0(gi, slot, j):
                b = WQ + (j % 2) * BANK
                dve.wait_ge(gathered, 1)
                dve.sem_inc(gathered, -1)
                dve.wait_ge(wq_ready, 1)
                dve.sem_inc(wq_ready, -1)
                rows = ring[:, ds(slot * G, G), :]
                g3 = lambda t: t[:].rearrange("p (g d) -> p g d", d=D)
                link(v.tensor_tensor(g3(t1), ps[:, b:b + G * D].rearrange("p (g d) -> p g d", d=D), rows[:, :, 0:D], ALU.mult))
                link(v.tensor_tensor(t2[:], ps[:, b + G * D:b + 2 * G * D], t1[:], ALU.mult))
                dve.sem_inc(wq_free, 1)
                link(v.tensor_reduce(al[:], t2[:].rearrange("p (a c) -> p a c", c=HD), AX.X, ALU.add))
                link(v.tensor_tensor(alw[:].rearrange("p (g h) -> p g h", h=HEADS),
                                     al[:].rearrange("p (g h) -> p g h", h=HEADS),
                                     ew_e[:, ds(gi * G, G)].unsqueeze(2).to_broadcast([P, G, HEADS]), ALU.mult))
                v.tensor_tensor(msg[:, j, 0:G * D].rearrange("p (g h c) -> p g h c", g=G, c=HD),
                                rows[:, :, D:2 * D].rearrange("p g (h c) -> p g h c", c=HD),
                                alw[:].rearrange("p (g h) -> p g h", h=HEADS).unsqueeze(3).to_broadcast([P, G, HEADS, HD]),
                                ALU.mult).then_inc(msg_ready, 1)

            dve.sem_inc(oh_free, STEPS)
            dve.sem_inc(wq_free, 2)
            RB = RG // STEPS

            def run0():
                for j in range(STEPS):
                    make0(0, j)
                    if j:
                        edges0(j - 1, j - 1, j - 1)
                with dve.Fori(1, RB) as it:
                    for j in range(STEPS):
                        make0(it, j)
                        edges0(it * STEPS + j - 1, it * STEPS + j - 1, (j - 1) % STEPS)
                with dve.Fori(1, NI // RING) as turn:
                    for j in range(STEPS):
                        it = turn * RB
                        make0(it, j)
                        edges0(it * STEPS + j - 1, RG - 1 if j == 0 else j - 1, (j - 1) % STEPS)
                    with dve.Fori(1, RB) as r:
                        for j in range(STEPS):
                            it = turn * RB + r
                            make0(it, j)
                            edges0(it * STEPS + j - 1, r * STEPS + j - 1, (j - 1) % STEPS)
                edges0(NG - 1, RG - 1, STEPS - 1)

            run0()

            def layer_norm(dst, srcv):
                s3 = lambda t: t.rearrange("p (t d) -> p t d", d=D)
                bc = lambda t: t.unsqueeze(2).to_broadcast([P, NT, D])
                link(v.tensor_reduce(stat[:, 0, :], s3(srcv), AX.X, ALU.add))
                link(v.tensor_scalar(stat[:, 0, :], stat[:, 0, :], 1.0 / D, None, ALU.mult))
                link(v.tensor_tensor(s3(srcv), s3(srcv), bc(stat[:, 0, :]), ALU.subtract))
                sq = h_in[:, 0:NT * D]
                link(v.tensor_tensor(sq, srcv, srcv, ALU.mult))
                link(v.tensor_reduce(stat[:, 1, :], s3(sq), AX.X, ALU.add))
                v.tensor_scalar(stat[:, 1, :], stat[:, 1, :], 1.0 / D, EPS, ALU.mult, ALU.add).then_inc(var_ready, 1)
                dve.wait_ge(sd_ready, 1)
                dve.sem_inc(sd_ready, -1)
                link(v.reciprocal(stat[:, 3, :], stat[:, 2, :]))
                return v.tensor_tensor(s3(dst), s3(srcv), bc(stat[:, 3, :]), ALU.mult)

            dve.wait_ge(oh_free, STEPS)
            link(v.tensor_tensor(t_a, ps[:, 0:NT * D], x1[:], ALU.add))
            dve.sem_inc(acc_free, 1)
            link(layer_norm(x1[:], t_a))

            for layer in range(2):
                dve.sem_inc(in_ready, 1)
                stage_tiles(x1 if layer == 0 else h_in, D if layer == 0 else P)
                dve.wait_ge(proj_done, 1)
                dve.sem_inc(proj_done, -1)
                n = NT * H
                r0, r1 = res[:, 0, :], res[:, 1, :]
                a_src = asd[:, :, 0:H].rearrange("p t h -> p h t")
                link(split3(a_src, [as3[:, s, :, :] for s in range(3)],
                            r0[:, 0:n].rearrange("p (h t) -> p h t", h=H), r1[:, 0:n].rearrange("p (h t) -> p h t", h=H)))
                split3(asd[:, :, H:2 * H], [ad3[:, s, :].rearrange("p (t h) -> p t h", h=H) for s in range(3)],
                       r0[:, 0:n].rearrange("p (t h) -> p t h", h=H), r1[:, 0:n].rearrange("p (t h) -> p t h", h=H)
                       ).then_inc(parts_ready, 1)
                dve.sem_inc(sel_free, 2)
                v.memset(l_e[:, :, NI:NIP], 0.0)

                def make1(hb):
                    dve.wait_ge(bd_ready[hb], 32)
                    dve.sem_inc(bd_ready[hb], -32)
                    for o in range(2):
                        v.tensor_scalar(oh_n[:, 2 * hb + o, :], bc_d[:, hb, o * G * P:(o + 1) * G * P], iota_p[:, 0:1],
                                        None, ALU.is_equal)
                    v.tensor_scalar(bc_s[:, hb, :], bc_s[:, hb, :], iota_p[:, 0:1], None, ALU.is_equal
                                    ).then_inc(sel_oh, 1)

                def edges1(c8, hb):
                    b = WQ + hb * BANK
                    link(v.tensor_tensor(oh_hi[:, hb, :].rearrange("p (g t) -> p g t", t=NT),
                                         hi_e[:, ds(c8 * 8, 8)].unsqueeze(2).to_broadcast([P, 8, NT]),
                                         iota_t[:].unsqueeze(1).to_broadcast([P, 8, NT]), ALU.is_equal))
                    dve.wait_ge(sel_mm, 1)
                    dve.sem_inc(sel_mm, -1)
                    dve.sem_inc(bd_free, 1)
                    link(v.tensor_tensor(sel[:].rearrange("p (g h t) -> p g h t", g=8, h=H),
                                         ps[:, b:b + 8 * H * NT].rearrange("p (g h t) -> p g h t", g=8, h=H),
                                         oh_hi[:, hb, :].rearrange("p (g t) -> p g t", t=NT).unsqueeze(2)
                                         .to_broadcast([P, 8, H, NT]), ALU.mult))
                    link(v.tensor_reduce(as_g[:], sel[:].rearrange("p (a t) -> p a t", t=NT), AX.X, ALU.add))
                    link(v.tensor_tensor(l_e[:, :, ds(c8 * 8, 8)], as_g[:].rearrange("p (g h) -> p h g", h=H),
                                         ps[:, b + 8 * H * NT:b + 8 * H * NT + 8 * H].rearrange("p (g h) -> p h g", h=H),
                                         ALU.add))
                    dve.sem_inc(sel_free, 1)

                make1(0)
                make1(1)
                edges1(0, 0)
                with dve.Fori(1, NB) as it:
                    make1(0)
                    edges1(it * 2 - 1, 1)
                    make1(1)
                    edges1(it * 2, 0)
                edges1(2 * NB - 1, 1)
                v.scalar_tensor_tensor(l_e[:], l_e[:], 0.2, l_e[:], ALU.mult, ALU.max).then_inc(lrow_ready, 1)
                dve.wait_ge(gathered, 1)
                for h in range(H):
                    dve.wait_ge(lrow_mm, 1)
                    dve.sem_inc(lrow_mm, -1)
                    link(v.tensor_copy(l_r[:, h, :], ps[:, 2 * h * BANK:2 * h * BANK + NIP]))
                for h in range(H):
                    lr = l_r[:, h, :]
                    fw, bw, mx = l_e[:, h, :], p_e[:, h, :], tmp_r[:].rearrange("p k e -> p (k e)")
                    v.tensor_tensor_scan(fw, keep_f[:].rearrange("p k e -> p (k e)"), lr, -BIG, ALU.add, ALU.max)
                    link(v.tensor_tensor_scan(bw[:, ::-1], keep_b[:].rearrange("p k e -> p (k e)")[:, ::-1], lr[:, ::-1],
                                              -BIG, ALU.add, ALU.max))
                    v.tensor_tensor(mx, fw, bw, ALU.max)
                    link(to_rows(ends, fw.rearrange("p (k e) -> p k e", e=P)[:, :, P - 1],
                                 bw.rearrange("p (k e) -> p k e", e=P)[:, :, 0]))
                    v.tensor_tensor_scan(runs[:, 0, :], links[:, 0, :], ends[:, 0, :], -BIG, ALU.add, ALU.max)
                    link(v.tensor_tensor_scan(runs[:, 1, ::-1], links[:, 1, ::-1], ends[:, 1, ::-1], -BIG,
                                              ALU.add, ALU.max))
                    v.memset(carry[:, 0, 0:1], -BIG)
                    v.memset(carry[:, 1, R - 1:R], -BIG)
                    v.tensor_tensor(carry[:, 0, 1:R], runs[:, 0, 0:R - 1], links[:, 2, 1:R], ALU.add)
                    v.tensor_tensor(carry[:, 1, 0:R - 1], runs[:, 1, 1:R], links[:, 3, 0:R - 1], ALU.add
                                    ).then_inc(carry_ready, 1)
                    dve.wait_ge(carry_mm, 1)
                    dve.sem_inc(carry_mm, -1)
                    link(v.tensor_copy(carry_c[:], ps[:, 0:2 * KB]))
                    for k in range(KB):
                        m_k = mx[:, k * P:(k + 1) * P]
                        last = v.scalar_tensor_tensor(m_k, not_first[:, k, :], carry_c[:, k:k + 1], m_k, ALU.add, ALU.max)
                    link(last)
                    for k in range(KB):
                        m_k = mx[:, k * P:(k + 1) * P]
                        last = v.scalar_tensor_tensor(m_k, not_last[:, k, :], carry_c[:, KB + k:KB + k + 1], m_k,
                                                      ALU.add, ALU.max)
                    link(last)
                    v.tensor_tensor(lr, lr, mx, ALU.subtract).then_inc(shift_ready, 1)
                    dve.sem_inc(tr_ready, 1)
                    dve.wait_ge(tr_mm, 1)
                    dve.sem_inc(tr_mm, -1)
                    link(v.tensor_tensor(l_e[:, h, :], ps[:, 2 * BANK:2 * BANK + NIP], ind_e, ALU.mult))
                    dve.wait_ge(prow_mm, 1)
                    dve.sem_inc(prow_mm, -1)
                    link(v.tensor_copy(p_e[:, h, :], ps[:, 0:NIP]))
                dve.sem_inc(acc_free, 1)

                with dve.Fori(0, NI // RING) as turn:
                    with dve.Fori(0, RG // STEPS) as r:
                        for j in range(STEPS):
                            dve.wait_ge(oh_free, 1)
                            dve.sem_inc(oh_free, -1)
                            at = turn * RING + r * BODY + j * G
                            for i in range(G):
                                v.tensor_scalar(oh_e[:, j, i * P:(i + 1) * P], iota_f[:], dl_e[:, ds(at + i, 1)],
                                                None, ALU.is_equal)
                            dve.wait_ge(gathered, 1)
                            dve.sem_inc(gathered, -1)
                            v.tensor_tensor(msg[:, j, :].rearrange("p (g h c) -> p g h c", g=G, h=H),
                                            ring[:, ds(r * BODY + j * G, G), :].rearrange("p g (h c) -> p g h c", h=H),
                                            p_e[:, :, ds(at, G)].rearrange("p h g -> p g h").unsqueeze(3)
                                            .to_broadcast([P, G, H, C]), ALU.mult).then_inc(msg_ready, 1)
                th = lambda q: node_m[:, q, :].rearrange("p (t h) -> p t h", h=H)
                sums = ps[:, SUMS:SUMS + NT * NX].rearrange("p (t q) -> p t q", q=NX)
                link(v.tensor_tensor(th(0), asd[:, :, 0:H], asd[:, :, H:2 * H], ALU.add))
                link(v.scalar_tensor_tensor(th(0), th(0), 0.2, th(0), ALU.mult, ALU.max))
                dve.wait_ge(oh_free, STEPS)
                link(v.tensor_scalar(th(1), sums[:, :, 2 * H:2 * H + 1].to_broadcast([P, NT, H]), -1.0, BIG,
                                     ALU.add, ALU.mult))
                link(v.tensor_tensor(th(1), sums[:, :, H:2 * H], th(1), ALU.add))
                link(v.tensor_tensor(th(4), th(0), th(1), ALU.max))
                v.tensor_tensor(th(2), th(1), th(4), ALU.subtract)
                v.tensor_tensor(th(3), th(0), th(4), ALU.subtract).then_inc(shift_ready, 1)
                dve.wait_ge(exp_nodes, 1)
                dve.sem_inc(exp_nodes, -1)
                link(v.tensor_tensor(th(0), sums[:, :, 0:H], th(4), ALU.mult))
                link(v.tensor_tensor(th(0), th(0), th(5), ALU.add))
                link(v.reciprocal(th(1), th(0)))
                link(v.tensor_tensor(node_m[:, 2:4, :], node_m[:, 4:6, :],
                                     node_m[:, 1:2, :].to_broadcast([P, 2, NT * H]), ALU.mult))
                spread = lambda q: node_m[:, q, :].unsqueeze(2).to_broadcast([P, NT * H, C])
                ac = lambda w_: w_.rearrange("p (a c) -> p a c", c=C)
                num = edge_x[:, 0:NT * H * C]
                v.tensor_tensor(ac(num), ac(ps[:, 0:NT * H * C]), spread(2), ALU.mult)
                link(v.tensor_tensor(ac(h_in[:]), ac(h_in[:]), spread(3), ALU.mult))
                dve.sem_inc(acc_free, 1)
                link(v.tensor_tensor(h_in[:], h_in[:], num, ALU.add))
                if layer == 0:
                    hv = h_in[:].rearrange("p (t f) -> p t f", f=H * C)
                    link(v.tensor_tensor(hv, hv, b1_b[:].unsqueeze(1).to_broadcast([P, NT, H * C]), ALU.add))
            hv = h_in[:].rearrange("p (t h c) -> p t h c", h=H, c=C)
            ta = t_a.rearrange("p (t d) -> p t d", d=D)
            link(v.tensor_tensor(ta, hv[:, :, 0, :], hv[:, :, 1, :], ALU.add))
            link(v.scalar_tensor_tensor(ta, ta, 1.0 / H, b2_b[:].unsqueeze(1).to_broadcast([P, NT, D]), ALU.mult, ALU.add))
            link(v.tensor_tensor(t_a, t_a, x1[:], ALU.add))
            layer_norm(t_a, t_a).then_inc(out_ready, 1)

        @block.tensor
        def _(pe):
            t = nc.tensor
            pe.wait_ge(consts_f, 1)
            pe.wait_ge(cnt_ready, 1)
            pe.sem_inc(cnt_ready, -1)
            t.matmul(ps[:, 0:NT - 1], ones[:], cnt[:], start=True, stop=True).then_inc(cs_ready, 1)
            pe.wait_ge(tc_ready, 1)
            pe.sem_inc(tc_ready, -1)

            def columns_to_rows(a_, b_):
                for k in range(KB):
                    t.matmul(ps[0:1, k * P:(k + 1) * P], a_[:, k:k + 1], ident[:], start=True, stop=True)
                for k in range(KB):
                    last = t.matmul(ps[0:1, 2 * BANK + k * P:2 * BANK + (k + 1) * P], b_[:, k:k + 1], ident[:],
                                    start=True, stop=True)
                return last

            columns_to_rows(t_col, c_col).then_inc(tcrow_mm, 1)
            pe.wait_ge(tr_done, 1)
            pe.sem_inc(tr_done, -1)
            pe.sem_inc(items_ready, 1)

            def project(width, rhs, n):
                with pe.Fori(0, NT // TG) as i:
                    pe.wait_ge(stage_ready, 1)
                    pe.sem_inc(stage_ready, -1)
                    pe.wait_ge(proj_free, 1)
                    pe.sem_inc(proj_free, -1)
                    for q in range(TG):
                        last = t.transpose(ps[0:width, q * P:(q + 1) * P], stage[:, q * width:(q + 1) * width], ident[:])
                    last.then_inc(stage_mm, 1)
                    pe.wait_ge(xT_ready, 1)
                    pe.sem_inc(xT_ready, -1)
                    pe.sem_inc(in_ready, 1)
                    for q in range(TG):
                        o = 2 * BANK + q * 256
                        last = t.matmul(ps[:, o:o + n], xT[0:width, q * P:(q + 1) * P], rhs, start=True, stop=True)
                    last.then_inc(proj_mm, 1)
                pe.wait_ge(in_ready, 1)
                pe.sem_inc(in_ready, -1)

            pe.wait_ge(weights_in, 16 * N_WEIGHTS)
            pe.sem_inc(proj_free, 1)
            project(D, w_qkv[:], 3 * D)
            def rows_to_columns():
                pe.wait_ge(tr_ready, 1)
                pe.sem_inc(tr_ready, -1)
                for k in range(KB):
                    last = t.transpose(ps[:, 2 * BANK + k * P:2 * BANK + (k + 1) * P], tmp_r[:, k, :], ident[:])
                last.then_inc(tr_mm, 1)

            def carries_to_columns():
                pe.wait_ge(carry_ready, 1)
                pe.sem_inc(carry_ready, -1)
                for q in range(2):
                    for k in range(KB):
                        last = t.matmul(ps[:, q * KB + k:q * KB + k + 1], ends[0:1, q, k * P:(k + 1) * P],
                                        ones[0:1, 0:1], start=True, stop=True)
                last.then_inc(carry_mm, 1)

            pe.wait_ge(proj_free, 1)
            pe.sem_inc(proj_free, -1)
            for n in range(4):
                rows_to_columns()
            pe.wait_ge(ends_ready, 1)
            pe.sem_inc(ends_ready, -1)
            columns_to_rows(carry_c[:, 0:KB], carry_c[:, KB:2 * KB]).then_inc(ends_mm, 1)
            carries_to_columns()
            rows_to_columns()
            pe.wait_ge(parts_ready, 1)
            pe.sem_inc(parts_ready, -1)

            def zero(n_banks):
                for b in range(n_banks):
                    last = t.matmul(ps[:, b * BANK:(b + 1) * BANK], zeros_bf[0:1, 0:P], zeros_bf[:], start=True, stop=True)
                return last

            def hidden(gb):
                pe.wait_ge(at_ready[gb], 16 * G)
                pe.sem_inc(at_ready[gb], -(16 * G))
                t.matmul(ps[:, HID + gb * BANK:HID + (gb + 1) * BANK], w_in[:], attrs_t[:, gb, :], start=True, stop=True
                         ).then_inc(hid_mm, 1)

            def edge_weights(gi, j):
                b = WQ + (j % 2) * BANK
                pe.wait_ge(wq_free, 1)
                pe.sem_inc(wq_free, -1)
                pe.wait_ge(hs_ready, 1)
                pe.sem_inc(hs_ready, -1)
                t.matmul(ps[:, b:b + G * D], ones[0:1, :], b_out[:].rearrange("a g d -> a (g d)"), start=True, stop=False,
                         skip_group_check=True)
                for i in range(G):
                    last = t.matmul(ps[:, b + i * D:b + (i + 1) * D], hid_s[:, j % 2, i * P:(i + 1) * P], w_out[:],
                                    start=False, stop=True, skip_group_check=True)
                last.then_inc(hs_free, 1)
                tiles = load_regs(ET.PE, t_row, gi * G, G, NT - 1)
                pe.wait_ge(ohn_ready, 1)
                pe.sem_inc(ohn_ready, -1)
                if j % 2 == 1:
                    pe.sem_inc(bd_free, 1)
                for i in range(G):
                    o = b + G * D + i * D
                    for s in range(3):
                        last = t.matmul(ps[:, o:o + D], oh_n[:, j, i * P:(i + 1) * P], part3[:, s, ds(tiles[i] * D, D)],
                                        start=(s == 0), stop=(s == 2), skip_group_check=True)
                last.then_inc(wq_ready, 1)

            def scatter0(gi, j):
                pe.wait_ge(msg_ready, 1)
                pe.sem_inc(msg_ready, -1)
                pe.sem_inc(ring_free, 1)
                tiles = load_regs(ET.PE, t_row, gi * G, G, NT - 1)
                for i in range(G):
                    last = t.matmul(ps[:, ds(tiles[i] * D, D)], oh_e[:, j, i * P:(i + 1) * P], msg[:, j, i * D:(i + 1) * D],
                                    start=False, stop=True, skip_group_check=True)
                last.then_inc(oh_free, 1)

            pe.sem_inc(bd_free, 2)
            pe.sem_inc(hs_free, 2)
            for j in range(STEPS):
                hidden(j % 2)
                if j == 0:
                    pe.wait_ge(ohn_ready, 1)
                    pe.sem_inc(ohn_ready, -1)
                    pe.sem_inc(ohn_ready, 1)
                    zero(4)
                if j >= 1:
                    edge_weights(j - 1, j - 1)
                if j >= 2:
                    scatter0(j - 2, j - 2)
            with pe.Fori(1, NB) as it:
                for j in range(STEPS):
                    hidden(j % 2)
                    edge_weights(it * STEPS + j - 1, (j - 1) % STEPS)
                    scatter0(it * STEPS + j - 2, (j - 2) % STEPS)
            edge_weights(NG - 1, STEPS - 1)
            scatter0(NG - 2, STEPS - 2)
            scatter0(NG - 1, STEPS - 1)

            pe.wait_ge(acc_free, 1)
            pe.sem_inc(acc_free, -1)
            pe.sem_inc(proj_free, 1)
            for layer in range(2):
                project(D if layer == 0 else P, w1x[:] if layer == 0 else w2x[:], H * C + 4)
                pe.wait_ge(parts_ready, 1)
                pe.sem_inc(parts_ready, -1)

                def select(c8, hb):
                    b = WQ + hb * BANK
                    pe.wait_ge(sel_free, 1)
                    pe.sem_inc(sel_free, -1)
                    pe.wait_ge(sel_oh, 1)
                    pe.sem_inc(sel_oh, -1)
                    tiles = load_regs(ET.PE, t_row, c8 * 8, 8, NT - 1)
                    for i in range(8):
                        o = b + i * H * NT
                        for s in range(3):
                            t.matmul(ps[:, o:o + H * NT], bc_s[:, hb, i * P:(i + 1) * P],
                                     as3[:, s, :, :].rearrange("p h t -> p (h t)"), start=(s == 0), stop=(s == 2))
                    for i in range(8):
                        o = b + 8 * H * NT + i * H
                        for s in range(3):
                            last = t.matmul(ps[:, o:o + H], oh_n[:, 2 * hb + i // 4, (i % 4) * P:(i % 4 + 1) * P],
                                            ad3[:, s, ds(tiles[i] * H, H)], start=(s == 0), stop=(s == 2))
                    last.then_inc(sel_mm, 1)

                with pe.Fori(0, NB) as it:
                    for hb in range(2):
                        select(it * 2 + hb, hb)
                pe.wait_ge(sel_free, 2)
                pe.sem_inc(sel_free, -2)
                pe.wait_ge(lrow_ready, 1)
                pe.sem_inc(lrow_ready, -1)
                for h in range(H):
                    for k in range(KB):
                        last = t.transpose(ps[:, (2 * h) * BANK + k * P:(2 * h) * BANK + (k + 1) * P],
                                           l_e[:, h, k * P:(k + 1) * P], ident[:])
                    last.then_inc(lrow_mm, 1)
                for h in range(H):
                    pe.wait_ge(ends_ready, 1)
                    pe.sem_inc(ends_ready, -1)
                    columns_to_rows(carry_c[:, 0:KB], carry_c[:, KB:2 * KB]).then_inc(ends_mm, 1)
                    carries_to_columns()
                    rows_to_columns()
                    pe.wait_ge(exp_ready, 1)
                    pe.sem_inc(exp_ready, -1)
                    for k in range(KB):
                        last = t.transpose(ps[:, k * P:(k + 1) * P], l_r[:, h, k * P:(k + 1) * P], ident[:])
                    last.then_inc(prow_mm, 1)
                pe.wait_ge(acc_free, 1)
                pe.sem_inc(acc_free, -1)
                zero(7)

                with pe.Fori(0, NI // RING) as turn:
                    with pe.Fori(0, RG // STEPS) as r:
                        for j in range(STEPS):
                            pe.wait_ge(msg_ready, 1)
                            pe.sem_inc(msg_ready, -1)
                            pe.sem_inc(ring_free, 1)
                            at = turn * RING + r * BODY + j * G
                            tiles = load_regs(ET.PE, t_row, at, G, NT - 1)
                            for i in range(G):
                                o = i * P
                                t.matmul(ps[:, ds(tiles[i] * P, P)], oh_e[:, j, o:o + P], msg[:, j, o:o + P],
                                         start=False, stop=True, skip_group_check=True)
                                last = t.matmul(ps[:, ds(tiles[i] * NX + SUMS, NX)], oh_e[:, j, o:o + P],
                                                ex[:, :, ds(at + i, 1)], start=False, stop=True, skip_group_check=True)
                            last.then_inc(oh_free, 1)
                pe.wait_ge(acc_free, 1)
                pe.sem_inc(acc_free, -1)


N_WEIGHTS = 19


def kernel(**inputs):
    import numpy as np
    import concourse.bacc as bacc
    from concourse.bass_utils import run_bass_kernel_spmd as run

    def rows(a, pad):
        full = np.full((NIP * P,), pad, a.dtype)
        full[:E] = a
        return full.reshape(NIP, P)

    a = {k: np.ascontiguousarray(v) for k, v in inputs.items()}
    attrs = np.zeros((F, EP), a["edge_attr_8"].dtype)
    attrs[:F8, :E] = a["edge_attr_8"].T
    attrs[F8:, :E] = a["edge_attr_16"].T
    arrays = {"x": a["x"], "src_rows": rows(a["src"], 0), "dst_rows": rows(a["dst"], DST_PAD),
              "ew_rows": rows(a["edge_weight"], 0), "attrs": attrs}
    for k in ("W_rad1", "b_rad1", "W_rad2", "b_rad2", "W_sph1", "b_sph1", "W_sph2", "b_sph2", "Wq", "Wk", "Wv"):
        arrays[k] = a["L0_gnn_" + k]
    for k in ("W1", "as1", "ad1", "b1", "W2", "as2", "ad2", "b2"):
        arrays[k] = a["L1_gnn_" + k]
    nc = bacc.Bacc("TRN2", target_bir_lowering=False, num_devices=1)
    args = [nc.dram_tensor(k, v.shape, mybir.dt.from_np(v.dtype), kind="ExternalInput").ap() for k, v in arrays.items()]
    out = nc.dram_tensor("out", (N, D), mybir.dt.float32, kind="ExternalOutput").ap()
    gnn(nc, *args, out)
    r = run(nc, [arrays], core_ids=[0])
    return r.results[0]["out"]
```

```python
import concourse.bass as bass
from concourse import mybir
from concourse.alu_op_type import AluOpType as ALU
from contextlib import ExitStack

P = 128
N, D, E = 3125, 64, 103125
NT = -(-N // P)
TAIL = N - (NT - 1) * P
NCH = -(-E // P)
G = 4
STEPS = 4
BODY = G * STEPS
NI = -(-(NCH + NT - 1) // BODY) * BODY
NB = NI // BODY
KB = -(-NI // P)
NIP = KB * P
NG = NI // G
RING = 7 * BODY
RG = RING // G
RB = RG // STEPS
TURNS = NI // RING
REST = NI % RING
F8, F16 = 8, 16
F = F8 + F16
EP = NIP * P
DST_PAD = 4095
HEADS, HD = 8, 8
NX = 5
H, C = 2, 64
AVG = 32.0
EPS = 1e-5
BIG = 2.0 ** 100
BANK = 512
TG = 5
PL = 65
NS = NT + 3


def gnn(nc, x, src_rows, dst_rows, ew_rows, attrs, w_rad1, b_rad1, w_rad2, b_rad2, w_sph1, b_sph1, w_sph2, b_sph2,
        wq, wk, wv, g1_w, g1_as, g1_ad, g1_b, g2_w, g2_as, g2_ad, g2_b, out):
    f32, bf16, i32 = mybir.dt.float32, mybir.dt.bfloat16, mybir.dt.int32
    ACT = mybir.ActivationFunctionType
    AX = mybir.AxisListType
    ET = mybir.EngineType
    ds = bass.ds
    ctx = ExitStack()
    with ctx:
        def sb(name, shape, dt=f32):
            return ctx.enter_context(nc.sbuf_tensor(name, shape, dt))

        def sem(name):
            return ctx.enter_context(nc.semaphore(name))

        table = nc.dram_tensor("table", [NT * P, P], f32, kind="Internal").ap()
        ds_dram = nc.dram_tensor("ds_dram", [NIP // 8, 2, 8 * P], bf16, kind="Internal").ap()

        iota_f = sb("iota_f", [P, P])
        iota_p = sb("iota_p", [P, 1])
        iota_t = sb("iota_t", [P, NT])
        tile_no = sb("tile_no", [P, NT - 1])
        item_no = sb("item_no", [P, KB])
        ident = sb("ident", [P, P])
        ones = sb("ones", [P, P])
        ones_bf = sb("ones_bf", [PL, P], bf16)
        iota_b = sb("iota_b", [P, P], bf16)
        zeros_bf = sb("zeros_bf", [1, BANK], bf16)
        w_in = sb("w_in", [F, P])
        b_in = sb("b_in", [P, 1])
        w_out = sb("w_out", [P, D])
        b_out2 = sb("b_out2", [PL, 2, D])
        b_part = sb("b_part", [PL, 3, D])
        b_out = sb("b_out", [PL, G, D], bf16)
        w_qkv = sb("w_qkv", [D, 3 * D])
        w1x = sb("w1x", [D, H * C + 4])
        w2x = sb("w2x", [P, H * C + 4])
        att = sb("att", [P, 4, H * C])
        att_prod = sb("att_prod", [P, H * C])
        b1_b = sb("b1_b", [P, H * C])
        b2_b = sb("b2_b", [P, C])
        x1 = sb("x1", [P, NT * D])
        h_in = sb("h_in", [P, NT * H * C])
        stat = sb("stat", [P, 4, NT])
        node_m = sb("node_m", [P, 6, NT * H])
        part3 = h_in[:, 0:3 * NT * D // 2].bitcast(bf16).rearrange("p (s n) -> p s n", s=3)
        asd = sb("asd", [P, NT, 4])
        res = sb("res", [P, 2, NT * 4])
        as3 = sb("as3", [P, 3, H, NT], bf16)
        ad3 = sb("ad3", [P, NT * H * 3], bf16)
        stage_xT = sb("stage_xT", [P, 2 * TG * P])
        stage, xT = stage_xT[:, 0:TG * P], stage_xT[:, TG * P:2 * TG * P]
        attrs_t = stage_xT[0:F, 0:2 * G * P].rearrange("p (b n) -> p b n", b=2)
        last_i = sb("last_i", [P, KB], i32)
        last_f = sb("last_f", [P, KB])
        cmp_a = sb("cmp_a", [P, KB * (NT - 1)])
        cnt = sb("cnt", [P, NT - 1])
        first_item = sb("first_item", [P, NT - 1])
        t_col = sb("t_col", [P, KB])
        t128 = sb("t128", [P, KB])
        c_col = sb("c_col", [P, KB])
        c_idx = sb("c_idx", [P, KB], i32)
        t_row = sb("t_row", [1, NIP], i32)
        c_row = sb("c_row", [1, NIP], i32)
        tmp_r = sb("tmp_r", [P, KB, P])
        src_e = sb("src_e", [P, NIP], i32)
        idx = sb("idx", [P, RING], i32)
        dl_e = sb("dl_e", [P, NIP])
        hi_e = sb("hi_e", [P, NIP])
        ew_e = sb("ew_e", [P, NIP])
        keep_f = sb("keep_f", [P, KB, P], bf16)
        keep_b = sb("keep_b", [P, KB, P], bf16)
        not_first = sb("not_first", [P, KB, P], bf16)
        not_last = sb("not_last", [P, KB, P], bf16)
        links = sb("links", [1, 4, NIP], bf16)
        carry_c = sb("carry_c", [P, 2 * KB])
        edge_x = sb("edge_x", [P, (H + NX) * NIP])
        l_r = edge_x[:, 0:H * NIP].rearrange("p (h n) -> p h n", h=H)
        ex = edge_x[:, H * NIP:(H + NX) * NIP].rearrange("p (q n) -> p q n", q=NX)
        p_e, l_e, ind_e = ex[:, 0:H, :], ex[:, H:2 * H, :], ex[:, 2 * H, :]
        t_a = edge_x[:, 2 * H * NIP:2 * H * NIP + NT * D]
        kv_rows = edge_x[:, 0:NT * P].rearrange("p (t f) -> p t f", f=P)
        ring = sb("ring", [P, RING, P])
        bc_d = sb("bc_d", [P, 2, 8 * P], bf16)
        bc_s = sb("bc_s", [P, 2, 8 * P], bf16)
        hid_s = bc_s[:].rearrange("p a n -> p (a n)").bitcast(f32).rearrange("p (a n) -> p a n", a=2)
        oh_n = sb("oh_n", [P, 4, G * P], bf16)
        work = sb("work", [P, 2 * STEPS, G * P])
        oh_e, msg = work[:, 0:STEPS, :], work[:, STEPS:2 * STEPS, :]
        oh_b = work[:, 0:STEPS // 2, :].rearrange("p a n -> p (a n)").bitcast(bf16).rearrange("p (j n) -> p j n", j=STEPS)
        msg3 = work[:, STEPS // 2:2 * STEPS, :].rearrange("p a n -> p (a n)").rearrange("p (j s n) -> p j s n", j=STEPS, s=3)
        top_half = lambda t: t.bitcast(bf16)[:, 1::2]
        bc_ds = work[:].rearrange("p a n -> p (a n)").bitcast(bf16).rearrange("p (b n) -> p b n", b=4)
        blk = lambda n: work[:, 2 * n:2 * n + 2, :].rearrange("p a n -> p (a n)")[:, 0:KB * P].rearrange("p (k e) -> p k e", e=P)
        src_r, dst_ri, ew_r, tmp_i = blk(0).bitcast(i32), blk(1).bitcast(i32), blk(2), blk(3).bitcast(i32)
        bf_r = [bc_s[:, n, 0:KB * P] for n in range(2)]
        dst_r = oh_n[:].rearrange("p a n -> p (a n)").bitcast(f32)[:, 0:NIP].rearrange("p (k e) -> p k e", e=P)
        w_rows = work[0:1].rearrange("p a n -> p (a n)")
        ends, runs = (w_rows[:, n * NIP:(n + 2) * NIP].rearrange("p (a n) -> p a n", a=2) for n in (0, 2))
        oh_hi = sb("oh_hi", [P, 2, 8 * NS], bf16)
        t12 = sb("t12", [P, 2 * G * D])
        t1, t2 = t12[:, 0:G * D], t12[:, G * D:2 * G * D]
        sel = [t12[:, 0:8 * H * NS], stage[:, 0:8 * H * NS]]
        first_silu = sb("first_silu", [1, 1])
        al = sb("al", [P, G * HEADS])
        alw = sb("alw", [P, G * HEADS])

        oh_n8 = lambda b: oh_n[:, 2 * b:2 * b + 2, :].rearrange("p a n -> p (a n)")
        hi8 = lambda b: oh_hi[:, b, :].rearrange("p (g t) -> p g t", t=NS)
        h_rows = h_in[:].rearrange("p (t f) -> p t f", f=P)

        ps = ctx.enter_context(nc.psum_tensor("ps", [P, 8 * BANK], f32))
        HID = 4 * BANK
        WQ = 6 * BANK
        SUMS = 6 * BANK + NT * H * C - 6 * BANK
        assert SUMS + NT * NX <= 7 * BANK

        consts_made = sem("consts_made")
        consts_f = sem("consts_f")
        weights_in = sem("weights_in")
        x_in = sem("x_in")
        last_in = sem("last_in")
        cnt_ready = sem("cnt_ready")
        cs_ready = sem("cs_ready")
        cidx_ready = sem("cidx_ready")
        tc_ready = sem("tc_ready")
        tcrow_mm = sem("tcrow_mm")
        rows_t = sem("rows_t")
        rows_gathered = sem("rows_gathered")
        bfrow_ready = sem("bfrow_ready")
        bfrow_out = sem("bfrow_out")
        tr_ready = sem("tr_ready")
        tr_mm = sem("tr_mm")
        tr_done = sem("tr_done")
        items_ready = sem("items_ready")
        chain = sem("chain")
        achain = sem("achain")
        zeroed = sem("zeroed")
        in_ready = sem("in_ready")
        stage_ready = sem("stage_ready")
        stage_mm = sem("stage_mm")
        xT_ready = sem("xT_ready")
        proj_mm = sem("proj_mm")
        proj_free = sem("proj_free")
        rows_ready = sem("rows_ready")
        rows_written = sem("rows_written")
        proj_done = sem("proj_done")
        parts_ready = sem("parts_ready")
        idx_staged = sem("idx_staged")
        g_sem = [sem(f"g_sem{i}") for i in range(4)]
        gathered = sem("gathered")
        ring_free = sem("ring_free")
        at_ready = [sem(f"at_ready{i}") for i in range(2)]
        at_free = sem("at_free")
        bd_ready = [sem(f"bd_ready{i}") for i in range(2)]
        bd_free = sem("bd_free")
        bc_ready = [sem(f"bc_ready{i}") for i in range(4)]
        bc_free = sem("bc_free")
        hi_made = sem("hi_made")
        chain_s = sem("chain_s")
        hid_mm = sem("hid_mm")
        hs_ready = sem("hs_ready")
        hs_free = sem("hs_free")
        ohn_ready = sem("ohn_ready")
        wq_ready = sem("wq_ready")
        wq_free = sem("wq_free")
        msg_ready = sem("msg_ready")
        oh_free = sem("oh_free")
        sel_oh = sem("sel_oh")
        sel_mm = sem("sel_mm")
        sel_free = sem("sel_free")
        lrow_ready = sem("lrow_ready")
        lrow_mm = sem("lrow_mm")
        ends_ready = sem("ends_ready")
        ends_mm = sem("ends_mm")
        carry_ready = sem("carry_ready")
        carry_mm = sem("carry_mm")
        shift_ready = sem("shift_ready")
        exp_ready = sem("exp_ready")
        prow_mm = sem("prow_mm")
        exp_nodes = sem("exp_nodes")
        p_ready = sem("p_ready")
        acc_free = sem("acc_free")
        var_ready = sem("var_ready")
        sd_ready = sem("sd_ready")
        out_ready = sem("out_ready")
        out_done = sem("out_done")

        def load_regs(engine, row, at, n, top):
            _, v = nc.values_load_multi_w_load_instructions(
                row[0:1, ds(at, n)], engines=[engine], min_val=0, max_val=top,
                skip_runtime_bounds_check_because="worked out as a count of at most that many")
            return v

        block = ctx.enter_context(nc.Block())

        @block.sync
        def _(sp):
            sp.dma_start(last_i[:], dst_rows.rearrange("(k p) e -> p k e", p=P)[:, :, P - 1],
                         allow_slow_non_contiguous=True).then_inc(last_in, 16)
            sp.dma_start(x1[:, 0:(NT - 1) * D].rearrange("p (t d) -> p t d", d=D),
                         x[0:(NT - 1) * P, :].rearrange("(t p) d -> p t d", p=P)).then_inc(x_in, 16)
            sp.wait_ge(consts_f, 1)
            sp.dma_start(x1[0:TAIL, (NT - 1) * D:NT * D], x[(NT - 1) * P:N, :]).then_inc(x_in, 16)
            n = 0
            for dst, s in ((w_in[0:F8, 0:D], w_rad1), (w_in[F8:F, D:2 * D], w_sph1),
                           (b_in[0:D, :], b_rad1.rearrange("(d a) -> d a", a=1)),
                           (b_in[D:P, :], b_sph1.rearrange("(d a) -> d a", a=1)),
                           (w_out[0:D, :], w_rad2), (w_out[D:P, :], w_sph2),
                           *((b_out2[32 * s:32 * s + 1, i, :], b.rearrange("(a d) -> a d", a=1))
                             for s in range(3) for i, b in enumerate((b_rad2, b_sph2))),
                           (w_qkv[:, 0:D], wq), (w_qkv[:, D:2 * D], wk), (w_qkv[:, 2 * D:3 * D], wv),
                           (w1x[:, 0:H * C], g1_w), (w2x[:, 0:H * C], g2_w),
                           (att[:, 0, :], g1_as.rearrange("h c -> (h c)").partition_broadcast(P)),
                           (att[:, 1, :], g1_ad.rearrange("h c -> (h c)").partition_broadcast(P)),
                           (att[:, 2, :], g2_as.rearrange("h c -> (h c)").partition_broadcast(P)),
                           (att[:, 3, :], g2_ad.rearrange("h c -> (h c)").partition_broadcast(P)),
                           (b1_b[:], g1_b.partition_broadcast(P)), (b2_b[:], g2_b.partition_broadcast(P))):
                sp.dma_start(dst, s).then_inc(weights_in, 16)
                n += 1
            assert n == N_WEIGHTS
            sp.wait_ge(bfrow_ready, 1)
            sp.sem_inc(bfrow_ready, -1)
            for k in range(KB):
                for s in range(2):
                    sp.dma_start(ds_dram[k * P // 8:(k + 1) * P // 8, s, :].rearrange("a (b e) -> a b e", e=P),
                                 bf_r[s][:, k * P:(k + 1) * P]).then_inc(bfrow_out, 16)

            def write_table(row_out):
                with sp.Fori(0, NT // TG) as i:
                    sp.wait_ge(rows_ready, 1)
                    sp.sem_inc(rows_ready, -1)
                    sp.dma_start(table.rearrange("(t p) f -> p t f", p=P)[:, ds(i * TG, TG), :],
                                 row_out[:, ds(i * TG, TG), :]).then_inc(rows_written, 16)

            write_table(kv_rows)
            sp.wait_ge(bfrow_out, 16 * 2 * KB)
            sp.wait_ge(items_ready, 1)
            sp.sem_inc(items_ready, -1)
            with sp.Fori(0, NB) as it:
                for hb in range(2):
                    sp.wait_ge(bd_free, 1)
                    sp.sem_inc(bd_free, -1)
                    sp.dma_start(bc_d[:, hb, :], ds_dram[ds(it * 2 + hb, 1), 0, :].rearrange("a e -> (a e)")
                                 .partition_broadcast(P)).then_inc(bd_ready[hb], 16)
                    cs = load_regs(ET.SP, c_row, it * BODY + hb * 8, 8, NIP - 1)
                    for gb in range(2):
                        sp.wait_ge(at_free, 1)
                        sp.sem_inc(at_free, -1)
                        for j in range(G):
                            sp.dma_start(attrs_t[:, gb, j * P:(j + 1) * P], attrs[:, ds(cs[gb * G + j] * P, P)]
                                         ).then_inc(at_ready[gb], 16)
            for layer in range(2):
                write_table(h_rows)
                with sp.Fori(0, NI // 32) as it:
                    for b in range(4):
                        sp.wait_ge(bc_free, 1)
                        sp.sem_inc(bc_free, -1)
                        sp.dma_start(bc_ds[:, b, :], ds_dram[ds(it * 4 + b, 1), :, :].rearrange("a s e -> (a s e)")
                                     .partition_broadcast(P)).then_inc(bc_ready[b], 16)
            sp.wait_ge(out_ready, 1)
            sp.sem_inc(out_ready, -1)
            sp.dma_start(out[0:(NT - 1) * P, :].rearrange("(t p) d -> p t d", p=P),
                         t_a[:, 0:(NT - 1) * D].rearrange("p (t d) -> p t d", d=D)).then_inc(out_done, 16)
            sp.dma_start(out[(NT - 1) * P:N, :], t_a[0:TAIL, (NT - 1) * D:NT * D]).then_inc(out_done, 16)
            sp.wait_ge(out_done, 32)

        @block.gpsimd
        def _(pool):
            g = nc.gpsimd
            g.iota(iota_f[:], [[1, P]], base=0, channel_multiplier=0, allow_small_or_imprecise_dtypes=True)
            g.iota(iota_p[:], [[1, 1]], base=0, channel_multiplier=1, allow_small_or_imprecise_dtypes=True)
            g.iota(iota_t[:], [[1, NT]], base=0, channel_multiplier=0, allow_small_or_imprecise_dtypes=True)
            g.iota(tile_no[:], [[1, NT - 1]], base=1, channel_multiplier=0, allow_small_or_imprecise_dtypes=True)
            g.iota(item_no[:], [[P, KB]], base=0, channel_multiplier=1,
                   allow_small_or_imprecise_dtypes=True).then_inc(consts_made, 1)
            pool.wait_ge(cidx_ready, 1)
            pool.sem_inc(cidx_ready, -1)
            for k in range(KB):
                for dst, rows in ((dst_ri, dst_rows), (src_r, src_rows), (ew_r, ew_rows)):
                    g.indirect_dma_start(dst[:, k, :], None, rows, bass.IndirectOffsetOnAxis(c_idx[:, k:k + 1], 0)
                                         ).then_inc(rows_gathered, 16)
            pool.sem_inc(ring_free, RG)
            pool.wait_ge(rows_t, 1)

            def pass_on(layer, turn, q):
                pool.wait_ge(g_sem[q % 4], layer * (16 * G * NG // 4) + turn * (16 * G * RG // 4) + 16 * G * (q // 4 + 1))
                pool.sem_inc(gathered, 1)

            def gather_turn(layer, turn, slots):
                for q in range(slots // G):
                    if q % 4 == 0:
                        s0 = q * G
                        g.tensor_copy(idx[:, s0:s0 + BODY], src_e[:, ds(turn * RING + s0, BODY)]
                                      ).then_inc(idx_staged, 1)
                        pool.wait_ge(idx_staged, 1)
                        pool.sem_inc(idx_staged, -1)
                    pool.wait_ge(ring_free, 1)
                    pool.sem_inc(ring_free, -1)
                    for j in range(G):
                        s = q * G + j
                        g.indirect_dma_start(ring[:, s, :], None, table, bass.IndirectOffsetOnAxis(idx[:, s:s + 1], 0)
                                             ).then_inc(g_sem[q % 4], 16)
                    if q >= 3:
                        pass_on(layer, turn, q - 3)
                for q in range(slots // G - 3, slots // G):
                    pass_on(layer, turn, q)

            with pool.Fori(0, 3) as layer:
                pool.wait_ge(rows_written, 16 * (NT // TG))
                pool.sem_inc(rows_written, -(16 * (NT // TG)))
                with pool.Fori(0, TURNS) as turn:
                    gather_turn(layer, turn, RING)
                gather_turn(layer, TURNS, REST)

        @block.scalar
        def _(act):
            a = nc.scalar

            def evacuate(width, row_out, first, n_side, side):
                with act.Fori(0, NT // TG) as i:
                    act.wait_ge(stage_mm, 1)
                    act.sem_inc(stage_mm, -1)
                    a.copy(xT[0:width, :], ps[0:width, 0:TG * P]).then_inc(xT_ready, 1)
                    act.wait_ge(proj_mm, 1)
                    act.sem_inc(proj_mm, -1)
                    pr = ps[:, 2 * BANK:2 * BANK + TG * 256].rearrange("p (t f) -> p t f", f=256)
                    a.copy(row_out[:, ds(i * TG, TG), :], pr[:, :, first:first + P]).then_inc(rows_ready, 1)
                    o = 0 if first else P
                    a.copy(side[:, ds(i * TG * n_side, TG * n_side)].rearrange("p (t f) -> p t f", f=n_side),
                           pr[:, :, o:o + n_side]).then_inc(proj_free, 1)
                act.drain().then_inc(proj_done, 1)

            def sqrt_var():
                act.wait_ge(var_ready, 1)
                act.sem_inc(var_ready, -1)
                a.activation(stat[:, 2, :], stat[:, 1, :], ACT.Sqrt).then_inc(sd_ready, 1)

            evacuate(D, kv_rows, D, D, t_a)

            def silu(gb):
                act.wait_ge(hid_mm, 1)
                act.sem_inc(hid_mm, -1)
                act.sem_inc(at_free, 1)
                act.wait_ge(hs_free, 1)
                act.sem_inc(hs_free, -1)
                a.activation(hid_s[:, gb, :], ps[:, HID + gb * BANK:HID + (gb + 1) * BANK], ACT.Silu,
                             bias=b_in[:, 0:1]).then_inc(hs_ready, 1)

            act.wait_ge(weights_in, 16 * N_WEIGHTS)
            act.sem_inc(at_free, 2)
            a.activation(first_silu[:], b_in[0:1, 0:1], ACT.Silu).then_inc(achain, 1)
            act.wait_ge(achain, 1)
            act.sem_inc(achain, -1)
            with act.Fori(0, NG // 2) as it:
                silu(0)
                silu(1)
            sqrt_var()
            for layer in range(2):
                evacuate(D if layer == 0 else P, h_rows, 0, 4, asd[:, :, :].rearrange("p t f -> p (t f)"))
                for h in range(H):
                    act.wait_ge(shift_ready, 1)
                    act.sem_inc(shift_ready, -1)
                    a.activation(l_r[:, h, :], l_r[:, h, :], ACT.Exp).then_inc(exp_ready, 1)
                act.wait_ge(shift_ready, 1)
                act.sem_inc(shift_ready, -1)
                a.activation(node_m[:, 4:6, :], node_m[:, 2:4, :], ACT.Exp).then_inc(exp_nodes, 1)
            sqrt_var()

        @block.vector
        def _(dve):
            v = nc.vector

            def link(ins, n=1):
                ins.then_inc(chain, 1)
                dve.wait_ge(chain, 1)
                dve.sem_inc(chain, -1)

            v.memset(x1[:, (NT - 1) * D:NT * D], 0.0)
            v.memset(w_in[:], 0.0)
            v.memset(b_out[:], 0.0)
            v.memset(b_out2[:], 0.0)
            v.memset(oh_hi[:], 1.0)
            v.memset(ones[:], 1.0)
            v.memset(ones_bf[:], 1.0)
            v.memset(zeros_bf[:], 0.0)
            v.memset(links[:], -BIG)
            v.memset(keep_f[:], -BIG)
            v.memset(keep_b[:], -BIG).then_inc(consts_f, 1)
            dve.wait_ge(consts_f, 1)
            dve.wait_ge(consts_made, 1)
            v.tensor_copy(iota_b[:], iota_f[:])
            link(v.tensor_scalar(ident[:], iota_f[:], iota_p[:, 0:1], None, ALU.is_equal))
            dve.wait_ge(last_in, 16)
            link(v.tensor_copy(last_f[:], last_i[:]))
            ca = cmp_a[:].rearrange("p (t k) -> p t k", k=KB)
            link(v.tensor_scalar(cnt[:], tile_no[:], float(P), None, ALU.mult))
            link(v.tensor_tensor(ca, last_f[:].unsqueeze(1).to_broadcast([P, NT - 1, KB]),
                                 cnt[:].unsqueeze(2).to_broadcast([P, NT - 1, KB]), ALU.is_lt))
            v.tensor_reduce(cnt[:], ca, AX.X, ALU.add).then_inc(cnt_ready, 1)
            dve.wait_ge(cs_ready, 1)
            dve.sem_inc(cs_ready, -1)
            link(v.tensor_tensor(first_item[:], ps[:, 0:NT - 1], tile_no[:], ALU.add))
            cb = cmp_a[:].rearrange("p (k t) -> p k t", k=KB)
            link(v.tensor_tensor(cb, first_item[:].unsqueeze(1).to_broadcast([P, KB, NT - 1]),
                                 item_no[:].unsqueeze(2).to_broadcast([P, KB, NT - 1]), ALU.is_le))
            link(v.tensor_reduce(t_col[:], cb, AX.X, ALU.add))
            link(v.tensor_tensor(c_col[:], item_no[:], t_col[:], ALU.subtract))
            v.tensor_copy(c_idx[:], c_col[:]).then_inc(cidx_ready, 1)
            v.tensor_scalar(t128[:], t_col[:], float(P), None, ALU.mult).then_inc(tc_ready, 1)
            dve.wait_ge(tcrow_mm, 1)
            dve.sem_inc(tcrow_mm, -1)
            v.tensor_copy(t_row[:], ps[0:1, 0:NIP])
            v.tensor_copy(c_row[:], ps[0:1, 2 * BANK:2 * BANK + NIP]).then_inc(tr_done, 1)
            dve.wait_ge(weights_in, 16 * N_WEIGHTS)
            link(v.tensor_tensor(b_part[:, 0, :], b_out2[:, 0, :], b_out2[:, 1, :], ALU.add))
            for s in range(2):
                link(v.tensor_tensor(b_part[:, s + 1, :], b_part[:, s, :], top_half(b_part[:, s, :]), ALU.subtract))
            for s in range(3):
                v.tensor_copy(b_out[32 * s:32 * s + 1, :, :],
                              top_half(b_part[32 * s:32 * s + 1, s, :]).unsqueeze(1).to_broadcast([1, G, D]))
            for wx, np_, first in ((w1x, D, 0), (w2x, P, 2)):
                for s in range(2):
                    link(v.tensor_tensor(att_prod[0:np_, :], wx[:, 0:H * C], att[0:np_, first + s, :], ALU.mult))
                    link(v.tensor_reduce(wx[:, H * C + 2 * s:H * C + 2 * s + 2],
                                         att_prod[0:np_, :].rearrange("p (h c) -> p h c", c=C), AX.X, ALU.add))

            def stage_tiles(inp, width):
                with dve.Fori(0, NT // TG) as i:
                    dve.wait_ge(in_ready, 1)
                    dve.sem_inc(in_ready, -1)
                    v.tensor_copy(stage[:, 0:TG * width], inp[:, ds(i * TG * width, TG * width)]
                                  ).then_inc(stage_ready, 1)

            dve.wait_ge(x_in, 32)
            dve.sem_inc(in_ready, 1)
            stage_tiles(x1, D)
            dve.wait_ge(proj_done, 1)
            dve.sem_inc(proj_done, -1)

            def split3(srcv, dst3, r0, r1):
                link(v.tensor_copy(dst3[0], srcv))
                link(v.tensor_tensor(r0, srcv, dst3[0], ALU.subtract))
                link(v.tensor_copy(dst3[1], r0))
                link(v.tensor_tensor(r1, r0, dst3[1], ALU.subtract))
                return v.tensor_copy(dst3[2], r1)

            hf = NT * D // 2
            for a0 in (0, hf):
                link(split3(t_a[:, a0:a0 + hf], [part3[:, s, a0:a0 + hf] for s in range(3)],
                            h_in[:, 3 * hf:4 * hf], tmp_r[:].rearrange("p k e -> p (k e)")[:, 0:hf]))

            dve.wait_ge(rows_gathered, 16 * 3 * KB)
            link(v.tensor_copy(dst_r[:], dst_ri[:]))
            for k in range(KB):
                last = v.tensor_scalar(tmp_r[:, k, :], dst_r[:, k, :], t128[:, k:k + 1], None, ALU.subtract)
            link(last)
            v.tensor_scalar(bf_r[0], tmp_r[:].rearrange("p k e -> p (k e)"), -1.0, float(P), ALU.max, ALU.min)
            link(v.tensor_scalar(tmp_i[:], src_r[:], P - 1, None, ALU.bitwise_and))
            v.tensor_copy(bf_r[1], tmp_i[:].rearrange("p k e -> p (k e)")).then_inc(bfrow_ready, 1)

            def to_edges(dst):
                dve.sem_inc(tr_ready, 1)
                dve.wait_ge(tr_mm, 1)
                dve.sem_inc(tr_mm, -1)
                return v.tensor_copy(dst, ps[:, 2 * BANK:2 * BANK + NIP])

            link(to_edges(dl_e[:]))
            link(v.tensor_copy(tmp_r[:], src_r[:]))
            to_edges(src_e[:]).then_inc(rows_t, 1)
            link(v.tensor_scalar(tmp_i[:], src_r[:], 7, None, ALU.logical_shift_right))
            link(v.tensor_copy(tmp_r[:], tmp_i[:]))
            link(to_edges(hi_e[:]))
            link(v.tensor_scalar(tmp_r[:], ew_r[:], 1.0 / (AVG * HD ** 0.5), None, ALU.mult))
            link(to_edges(ew_e[:]))

            def mask(dst, a_, b_):
                link(v.tensor_tensor(dst, a_, b_, ALU.not_equal))
                link(v.tensor_scalar(dst, dst, -BIG, None, ALU.mult))

            mask(keep_f[:, :, 1:P], dst_r[:, :, 1:P], dst_r[:, :, 0:P - 1])
            mask(keep_b[:, :, 0:P - 1], dst_r[:, :, 1:P], dst_r[:, :, 0:P - 1])
            for k in range(KB):
                v.tensor_scalar(not_first[:, k, :], dst_r[:, k, :], dst_r[:, k, 0:1], -BIG, ALU.not_equal, ALU.mult)
                last = v.tensor_scalar(not_last[:, k, :], dst_r[:, k, :], dst_r[:, k, P - 1:P], -BIG,
                                       ALU.not_equal, ALU.mult)
            link(last)

            def to_rows(dst, a_, b_):
                v.tensor_copy(carry_c[:, 0:KB], a_)
                v.tensor_copy(carry_c[:, KB:2 * KB], b_).then_inc(ends_ready, 1)
                dve.wait_ge(ends_mm, 1)
                dve.sem_inc(ends_mm, -1)
                v.tensor_copy(dst[:, 0, :], ps[0:1, 0:NIP])
                return v.tensor_copy(dst[:, 1, :], ps[0:1, 2 * BANK:2 * BANK + NIP])

            link(to_rows(ends, dst_r[:, :, 0], dst_r[:, :, P - 1]))
            carry = ends
            e0, e1 = ends[:, 0, :], ends[:, 1, :]
            R = NIP
            link(v.tensor_tensor(runs[:, 1, 0:R - 1], t_row[:, 1:R], t_row[:, 0:R - 1], ALU.not_equal))

            def link_mask(dst, a_, b_):
                link(v.tensor_tensor(runs[:, 0, 0:R - 1], a_, b_, ALU.not_equal))
                link(v.tensor_tensor(runs[:, 0, 0:R - 1], runs[:, 0, 0:R - 1], runs[:, 1, 0:R - 1], ALU.max))
                link(v.tensor_scalar(dst, runs[:, 0, 0:R - 1], -BIG, None, ALU.mult))

            link_mask(links[:, 0, 1:R], e1[:, 0:R - 1], e1[:, 1:R])
            link_mask(links[:, 1, 0:R - 1], e0[:, 1:R], e0[:, 0:R - 1])
            link_mask(links[:, 2, 1:R], e1[:, 0:R - 1], e0[:, 1:R])
            link_mask(links[:, 3, 0:R - 1], e0[:, 1:R], e1[:, 0:R - 1])
            v.memset(ends[:, :, R - 1:R], 1.0)
            v.tensor_copy(ends[:, 0, 0:R - 1], runs[:, 0, 0:R - 1]).then_inc(carry_ready, 1)
            dve.wait_ge(carry_mm, 1)
            dve.sem_inc(carry_mm, -1)
            link(v.tensor_tensor(tmp_r[:, :, 0:P - 1], dst_r[:, :, 1:P], dst_r[:, :, 0:P - 1], ALU.not_equal))
            link(v.tensor_copy(tmp_r[:, :, P - 1], ps[:, 0:KB]))
            link(to_edges(ind_e))
            dve.sem_inc(parts_ready, 1)

            def one_hot_nodes(o, hb, half):
                return v.tensor_scalar(oh_n[:, o, :], bc_d[:, hb, half * G * P:(half + 1) * G * P], iota_p[:, 0:1],
                                       None, ALU.is_equal)

            def step0(gi, slot, j, make=None, finish=True, chain_on=True):
                b = WQ + (j % 2) * BANK
                jn, jp = (j + 1) % STEPS, (j - 1) % STEPS
                g3 = lambda t: t.rearrange("p (g d) -> p g d", d=D)
                rows = ring[:, ds(slot * G, G), :] if chain_on else None
                rest = lambda q: v.tensor_tensor(msg3[:, jp, q + 1, :], msg3[:, jp, q, :],
                                                 top_half(msg3[:, jp, q, :]), ALU.subtract)
                if chain_on:
                    dve.wait_ge(gathered, 1)
                    dve.sem_inc(gathered, -1)
                    dve.wait_ge(wq_ready, 1)
                    dve.sem_inc(wq_ready, -1)
                    v.tensor_tensor(g3(t1), g3(ps[:, b:b + G * D]), rows[:, :, 0:D], ALU.mult).then_inc(chain, 1)
                if finish:
                    dve.wait_ge(chain_s, 1)
                    dve.sem_inc(chain_s, -1)
                    dve.sem_inc(ring_free, 1)
                    rest(0).then_inc(chain_s, 1)
                if chain_on:
                    dve.wait_ge(chain, 1)
                    dve.sem_inc(chain, -1)
                    v.tensor_tensor(t2, ps[:, b + G * D:b + 2 * G * D], t1, ALU.mult).then_inc(chain, 1)
                if finish:
                    dve.wait_ge(chain_s, 1)
                    dve.sem_inc(chain_s, -1)
                    rest(1).then_inc(msg_ready, 1)
                if chain_on:
                    dve.wait_ge(chain, 1)
                    dve.sem_inc(chain, -1)
                    dve.sem_inc(wq_free, 1)
                    v.tensor_reduce(al[:], t2.rearrange("p (a c) -> p a c", c=HD), AX.X, ALU.add).then_inc(chain, 1)
                if make is not None:
                    dve.wait_ge(oh_free, 1)
                    dve.sem_inc(oh_free, -1)
                    if jn % 2 == 0:
                        dve.wait_ge(bd_ready[jn // 2], 16)
                        dve.sem_inc(bd_ready[jn // 2], -16)
                    one_hot_nodes(jn, jn // 2, jn % 2).then_inc(ohn_ready, 1)
                if chain_on:
                    dve.wait_ge(chain, 1)
                    dve.sem_inc(chain, -1)
                    v.tensor_tensor(alw[:].rearrange("p (g h) -> p g h", h=HEADS),
                                    al[:].rearrange("p (g h) -> p g h", h=HEADS),
                                    ew_e[:, ds(gi * G, G)].unsqueeze(2).to_broadcast([P, G, HEADS]), ALU.mult
                                    ).then_inc(chain, 1)
                if make is not None:
                    for i in range(G):
                        v.tensor_scalar(oh_b[:, jn, i * P:(i + 1) * P], iota_b[:],
                                        dl_e[:, ds(make * BODY + jn * G + i, 1)], None, ALU.is_equal)
                if chain_on:
                    dve.wait_ge(chain, 1)
                    dve.sem_inc(chain, -1)
                    v.tensor_tensor(msg3[:, j, 0, :].rearrange("p (g h c) -> p g h c", g=G, c=HD),
                                    rows[:, :, D:2 * D].rearrange("p g (h c) -> p g h c", c=HD),
                                    alw[:].rearrange("p (g h) -> p g h", h=HEADS).unsqueeze(3)
                                    .to_broadcast([P, G, HEADS, HD]), ALU.mult).then_inc(chain_s, 1)

            dve.sem_inc(oh_free, STEPS)
            dve.sem_inc(wq_free, 2)
            step0(None, None, STEPS - 1, make=0, finish=False, chain_on=False)
            for j in range(1, STEPS):
                step0(j - 1, j - 1, j - 1, make=0, finish=j > 1)
            with dve.Fori(1, RB) as it:
                for j in range(STEPS):
                    step0(it * STEPS + j - 1, it * STEPS + j - 1, (j - 1) % STEPS, make=it)

            def turn0(turn, bodies):
                for j in range(STEPS):
                    it = turn * RB
                    step0(it * STEPS + j - 1, RG - 1 if j == 0 else j - 1, (j - 1) % STEPS, make=it)
                with dve.Fori(1, bodies) as r:
                    for j in range(STEPS):
                        it = turn * RB + r
                        step0(it * STEPS + j - 1, r * STEPS + j - 1, (j - 1) % STEPS, make=it)

            with dve.Fori(1, TURNS) as turn:
                turn0(turn, RB)
            turn0(TURNS, REST // BODY)
            step0(NG - 1, REST // G - 1, STEPS - 1)
            step0(None, None, 0, chain_on=False)

            def layer_norm(dst, srcv):
                s3 = lambda t: t.rearrange("p (t d) -> p t d", d=D)
                bc = lambda t: t.unsqueeze(2).to_broadcast([P, NT, D])
                link(v.tensor_reduce(stat[:, 0, :], s3(srcv), AX.X, ALU.add))
                link(v.tensor_scalar(stat[:, 0, :], stat[:, 0, :], 1.0 / D, None, ALU.mult))
                link(v.tensor_tensor(s3(srcv), s3(srcv), bc(stat[:, 0, :]), ALU.subtract))
                sq = h_in[:, 0:NT * D]
                link(v.tensor_tensor(sq, srcv, srcv, ALU.mult))
                link(v.tensor_reduce(stat[:, 1, :], s3(sq), AX.X, ALU.add))
                v.tensor_scalar(stat[:, 1, :], stat[:, 1, :], 1.0 / D, EPS, ALU.mult, ALU.add).then_inc(var_ready, 1)
                dve.wait_ge(sd_ready, 1)
                dve.sem_inc(sd_ready, -1)
                link(v.reciprocal(stat[:, 3, :], stat[:, 2, :]))
                return v.tensor_tensor(s3(dst), s3(srcv), bc(stat[:, 3, :]), ALU.mult)

            dve.wait_ge(oh_free, STEPS)
            link(v.tensor_tensor(t_a, ps[:, 0:NT * D], x1[:], ALU.add))
            dve.sem_inc(acc_free, 1)
            link(layer_norm(x1[:], t_a))

            for layer in range(2):
                dve.sem_inc(in_ready, 1)
                stage_tiles(x1 if layer == 0 else h_in, D if layer == 0 else P)
                dve.wait_ge(proj_done, 1)
                dve.sem_inc(proj_done, -1)
                n = NT * H
                r0, r1 = res[:, 0, :], res[:, 1, :]
                a_src = asd[:, :, 0:H].rearrange("p t h -> p h t")
                link(split3(a_src, [as3[:, s, :, :] for s in range(3)],
                            r0[:, 0:n].rearrange("p (h t) -> p h t", h=H), r1[:, 0:n].rearrange("p (h t) -> p h t", h=H)))
                split3(asd[:, :, H:2 * H], [ad3[:].rearrange("p (t h s) -> p s t h", h=H, s=3)[:, s] for s in range(3)],
                       r0[:, 0:n].rearrange("p (t h) -> p t h", h=H), r1[:, 0:n].rearrange("p (t h) -> p t h", h=H)
                       ).then_inc(parts_ready, 1)
                dve.sem_inc(sel_free, 2)

                def make1(b, hb):
                    dve.wait_ge(bc_ready[b], 16)
                    dve.sem_inc(bc_ready[b], -16)
                    v.tensor_scalar(oh_n8(hb), bc_ds[:, b, 0:8 * P], iota_p[:, 0:1], None, ALU.is_equal)
                    v.tensor_scalar(bc_s[:, hb, :], bc_ds[:, b, 8 * P:16 * P], iota_p[:, 0:1], None, ALU.is_equal
                                    ).then_inc(sel_oh, 1)

                def tile_hot(c8, hb):
                    v.tensor_tensor(hi8(hb)[:, :, 0:NT],
                                    hi_e[:, ds(c8 * 8, 8)].unsqueeze(2).to_broadcast([P, 8, NT]),
                                    iota_t[:].unsqueeze(1).to_broadcast([P, 8, NT]), ALU.is_equal).then_inc(hi_made, 1)

                def pick(hb):
                    o = WQ + hb * BANK
                    dve.wait_ge(hi_made, 1)
                    dve.sem_inc(hi_made, -1)
                    dve.wait_ge(sel_mm, 1)
                    dve.sem_inc(sel_mm, -1)
                    v.tensor_tensor(sel[hb].rearrange("p (g h t) -> p g h t", g=8, h=H),
                                    ps[:, o:o + 8 * H * NS].rearrange("p (g h t) -> p g h t", g=8, h=H),
                                    hi8(hb).unsqueeze(2).to_broadcast([P, 8, H, NS]), ALU.mult).then_inc(chain, 1)

                def logits(c8, hb):
                    dve.wait_ge(chain, 1)
                    dve.sem_inc(chain, -1)
                    dve.sem_inc(sel_free, 1)
                    v.tensor_reduce(l_e[:, :, ds(c8 * 8, 8)], sel[hb].rearrange("p (g h t) -> p h g t", g=8, h=H),
                                    AX.X, ALU.add)

                def step1(c8, b):
                    pick(b % 2)
                    make1(b, b % 2)
                    logits(c8, b % 2)
                    tile_hot(c8 + 2, b % 2)

                dve.sem_inc(bc_free, 4)
                for hb in range(2):
                    make1(hb, hb)
                    tile_hot(hb, hb)
                for b in range(2, 4):
                    step1(b - 2, b)
                with dve.Fori(1, NI // 32) as it:
                    for b in range(4):
                        step1(it * 4 + b - 2, b)
                for hb in range(2):
                    pick(hb)
                    logits(NI // 8 - 2 + hb, hb)
                dve.wait_ge(bc_free, 4)
                dve.sem_inc(bc_free, -4)
                link(v.memset(l_e[:, :, NI:NIP], 0.0))
                v.scalar_tensor_tensor(l_e[:], l_e[:], 0.2, l_e[:], ALU.mult, ALU.max).then_inc(lrow_ready, 1)
                for h in range(H):
                    dve.wait_ge(lrow_mm, 1)
                    dve.sem_inc(lrow_mm, -1)
                    link(v.tensor_copy(l_r[:, h, :], ps[:, 2 * h * BANK:2 * h * BANK + NIP]))
                for h in range(H):
                    lr = l_r[:, h, :]
                    fw, bw, mx = l_e[:, h, :], p_e[:, h, :], tmp_r[:].rearrange("p k e -> p (k e)")
                    v.tensor_tensor_scan(fw, keep_f[:].rearrange("p k e -> p (k e)"), lr, -BIG, ALU.add, ALU.max)
                    link(v.tensor_tensor_scan(bw[:, ::-1], keep_b[:].rearrange("p k e -> p (k e)")[:, ::-1], lr[:, ::-1],
                                              -BIG, ALU.add, ALU.max))
                    v.tensor_tensor(mx, fw, bw, ALU.max)
                    link(to_rows(ends, fw.rearrange("p (k e) -> p k e", e=P)[:, :, P - 1],
                                 bw.rearrange("p (k e) -> p k e", e=P)[:, :, 0]))
                    v.tensor_tensor_scan(runs[:, 0, :], links[:, 0, :], ends[:, 0, :], -BIG, ALU.add, ALU.max)
                    link(v.tensor_tensor_scan(runs[:, 1, ::-1], links[:, 1, ::-1], ends[:, 1, ::-1], -BIG,
                                              ALU.add, ALU.max))
                    v.memset(carry[:, 0, 0:1], -BIG)
                    v.memset(carry[:, 1, R - 1:R], -BIG)
                    v.tensor_tensor(carry[:, 0, 1:R], runs[:, 0, 0:R - 1], links[:, 2, 1:R], ALU.add)
                    v.tensor_tensor(carry[:, 1, 0:R - 1], runs[:, 1, 1:R], links[:, 3, 0:R - 1], ALU.add
                                    ).then_inc(carry_ready, 1)
                    dve.wait_ge(carry_mm, 1)
                    dve.sem_inc(carry_mm, -1)
                    link(v.tensor_copy(carry_c[:], ps[:, 0:2 * KB]))
                    for k in range(KB):
                        m_k = mx[:, k * P:(k + 1) * P]
                        last = v.scalar_tensor_tensor(m_k, not_first[:, k, :], carry_c[:, k:k + 1], m_k, ALU.add, ALU.max)
                    link(last)
                    for k in range(KB):
                        m_k = mx[:, k * P:(k + 1) * P]
                        last = v.scalar_tensor_tensor(m_k, not_last[:, k, :], carry_c[:, KB + k:KB + k + 1], m_k,
                                                      ALU.add, ALU.max)
                    link(last)
                    v.tensor_tensor(lr, lr, mx, ALU.subtract).then_inc(shift_ready, 1)
                    dve.sem_inc(tr_ready, 1)
                    dve.wait_ge(tr_mm, 1)
                    dve.sem_inc(tr_mm, -1)
                    link(v.tensor_tensor(l_e[:, h, :], ps[:, 2 * BANK:2 * BANK + NIP], ind_e, ALU.mult))
                    dve.wait_ge(prow_mm, 1)
                    dve.sem_inc(prow_mm, -1)
                    link(v.tensor_copy(p_e[:, h, :], ps[:, 0:NIP]))
                dve.sem_inc(acc_free, 1)

                def messages(at, slot, j):
                    dve.wait_ge(oh_free, 1)
                    dve.sem_inc(oh_free, -1)
                    for i in range(G):
                        v.tensor_scalar(oh_e[:, j, i * P:(i + 1) * P], iota_f[:], dl_e[:, ds(at + i, 1)],
                                        None, ALU.is_equal)
                    dve.wait_ge(gathered, 1)
                    dve.sem_inc(gathered, -1)
                    v.tensor_tensor(msg[:, j, :].rearrange("p (g h c) -> p g h c", g=G, h=H),
                                    ring[:, ds(slot, G), :].rearrange("p g (h c) -> p g h c", h=H),
                                    p_e[:, :, ds(at, G)].rearrange("p h g -> p g h").unsqueeze(3)
                                    .to_broadcast([P, G, H, C]), ALU.mult).then_inc(msg_ready, 1)

                def turn1(turn, bodies):
                    with dve.Fori(0, bodies) as r:
                        for j in range(STEPS):
                            messages(turn * RING + r * BODY + j * G, r * BODY + j * G, j)

                with dve.Fori(0, TURNS) as turn:
                    turn1(turn, RB)
                turn1(TURNS, REST // BODY)
                th = lambda q: node_m[:, q, :].rearrange("p (t h) -> p t h", h=H)
                sums = ps[:, SUMS:SUMS + NT * NX].rearrange("p (t q) -> p t q", q=NX)
                link(v.tensor_tensor(th(0), asd[:, :, 0:H], asd[:, :, H:2 * H], ALU.add))
                link(v.scalar_tensor_tensor(th(0), th(0), 0.2, th(0), ALU.mult, ALU.max))
                dve.wait_ge(oh_free, STEPS)
                link(v.tensor_scalar(th(1), sums[:, :, 2 * H:2 * H + 1].to_broadcast([P, NT, H]), -1.0, BIG,
                                     ALU.add, ALU.mult))
                link(v.tensor_tensor(th(1), sums[:, :, H:2 * H], th(1), ALU.add))
                link(v.tensor_tensor(th(4), th(0), th(1), ALU.max))
                v.tensor_tensor(th(2), th(1), th(4), ALU.subtract)
                v.tensor_tensor(th(3), th(0), th(4), ALU.subtract).then_inc(shift_ready, 1)
                dve.wait_ge(exp_nodes, 1)
                dve.sem_inc(exp_nodes, -1)
                link(v.tensor_tensor(th(0), sums[:, :, 0:H], th(4), ALU.mult))
                link(v.tensor_tensor(th(0), th(0), th(5), ALU.add))
                link(v.reciprocal(th(1), th(0)))
                link(v.tensor_tensor(node_m[:, 2:4, :], node_m[:, 4:6, :],
                                     node_m[:, 1:2, :].to_broadcast([P, 2, NT * H]), ALU.mult))
                spread = lambda q: node_m[:, q, :].unsqueeze(2).to_broadcast([P, NT * H, C])
                ac = lambda w_: w_.rearrange("p (a c) -> p a c", c=C)
                num = edge_x[:, 0:NT * H * C]
                v.tensor_tensor(ac(num), ac(ps[:, 0:NT * H * C]), spread(2), ALU.mult)
                link(v.tensor_tensor(ac(h_in[:]), ac(h_in[:]), spread(3), ALU.mult))
                dve.sem_inc(acc_free, 1)
                link(v.tensor_tensor(h_in[:], h_in[:], num, ALU.add))
                if layer == 0:
                    hv = h_in[:].rearrange("p (t f) -> p t f", f=H * C)
                    link(v.tensor_tensor(hv, hv, b1_b[:].unsqueeze(1).to_broadcast([P, NT, H * C]), ALU.add))
            hv = h_in[:].rearrange("p (t h c) -> p t h c", h=H, c=C)
            ta = t_a.rearrange("p (t d) -> p t d", d=D)
            link(v.tensor_tensor(ta, hv[:, :, 0, :], hv[:, :, 1, :], ALU.add))
            link(v.scalar_tensor_tensor(ta, ta, 1.0 / H, b2_b[:].unsqueeze(1).to_broadcast([P, NT, D]), ALU.mult, ALU.add))
            link(v.tensor_tensor(t_a, t_a, x1[:], ALU.add))
            layer_norm(t_a, t_a).then_inc(out_ready, 1)

        @block.tensor
        def _(pe):
            t = nc.tensor
            pe.wait_ge(consts_f, 1)
            pe.wait_ge(cnt_ready, 1)
            pe.sem_inc(cnt_ready, -1)
            t.matmul(ps[:, 0:NT - 1], ones[:], cnt[:], start=True, stop=True).then_inc(cs_ready, 1)
            pe.wait_ge(tc_ready, 1)
            pe.sem_inc(tc_ready, -1)

            def columns_to_rows(a_, b_):
                for k in range(KB):
                    t.matmul(ps[0:1, k * P:(k + 1) * P], a_[:, k:k + 1], ident[:], start=True, stop=True)
                for k in range(KB):
                    last = t.matmul(ps[0:1, 2 * BANK + k * P:2 * BANK + (k + 1) * P], b_[:, k:k + 1], ident[:],
                                    start=True, stop=True)
                return last

            columns_to_rows(t_col, c_col).then_inc(tcrow_mm, 1)
            pe.wait_ge(tr_done, 1)
            pe.sem_inc(tr_done, -1)
            pe.sem_inc(items_ready, 1)

            def project(width, rhs, n):
                with pe.Fori(0, NT // TG) as i:
                    pe.wait_ge(stage_ready, 1)
                    pe.sem_inc(stage_ready, -1)
                    pe.wait_ge(proj_free, 1)
                    pe.sem_inc(proj_free, -1)
                    for q in range(TG):
                        last = t.transpose(ps[0:width, q * P:(q + 1) * P], stage[:, q * width:(q + 1) * width], ident[:])
                    last.then_inc(stage_mm, 1)
                    pe.wait_ge(xT_ready, 1)
                    pe.sem_inc(xT_ready, -1)
                    pe.sem_inc(in_ready, 1)
                    for q in range(TG):
                        o = 2 * BANK + q * 256
                        last = t.matmul(ps[:, o:o + n], xT[0:width, q * P:(q + 1) * P], rhs, start=True, stop=True)
                    last.then_inc(proj_mm, 1)
                pe.wait_ge(in_ready, 1)
                pe.sem_inc(in_ready, -1)

            pe.wait_ge(weights_in, 16 * N_WEIGHTS)
            pe.sem_inc(proj_free, 1)
            project(D, w_qkv[:], 3 * D)
            def rows_to_columns():
                pe.wait_ge(tr_ready, 1)
                pe.sem_inc(tr_ready, -1)
                for k in range(KB):
                    last = t.transpose(ps[:, 2 * BANK + k * P:2 * BANK + (k + 1) * P], tmp_r[:, k, :], ident[:])
                last.then_inc(tr_mm, 1)

            def carries_to_columns():
                pe.wait_ge(carry_ready, 1)
                pe.sem_inc(carry_ready, -1)
                for q in range(2):
                    for k in range(KB):
                        last = t.matmul(ps[:, q * KB + k:q * KB + k + 1], ends[0:1, q, k * P:(k + 1) * P],
                                        ones[0:1, 0:1], start=True, stop=True)
                last.then_inc(carry_mm, 1)

            pe.wait_ge(proj_free, 1)
            pe.sem_inc(proj_free, -1)
            for n in range(4):
                rows_to_columns()
            pe.wait_ge(ends_ready, 1)
            pe.sem_inc(ends_ready, -1)
            columns_to_rows(carry_c[:, 0:KB], carry_c[:, KB:2 * KB]).then_inc(ends_mm, 1)
            carries_to_columns()
            rows_to_columns()
            pe.wait_ge(parts_ready, 1)
            pe.sem_inc(parts_ready, -1)

            def zero(n_banks):
                for b in range(n_banks):
                    last = t.matmul(ps[:, b * BANK:(b + 1) * BANK], zeros_bf[0:1, 0:P], zeros_bf[:], start=True, stop=True)
                return last

            def hidden(gb):
                pe.wait_ge(at_ready[gb], 16 * G)
                pe.sem_inc(at_ready[gb], -(16 * G))
                t.matmul(ps[:, HID + gb * BANK:HID + (gb + 1) * BANK], w_in[:], attrs_t[:, gb, :], start=True, stop=True
                         ).then_inc(hid_mm, 1)

            def edge_weights(gi, j):
                b = WQ + (j % 2) * BANK
                pe.wait_ge(wq_free, 1)
                pe.sem_inc(wq_free, -1)
                pe.wait_ge(hs_ready, 1)
                pe.sem_inc(hs_ready, -1)
                t.matmul(ps[:, b:b + G * D], ones_bf[:], b_out[:].rearrange("a g d -> a (g d)"), start=True, stop=False,
                         skip_group_check=True)
                for i in range(G):
                    last = t.matmul(ps[:, b + i * D:b + (i + 1) * D], hid_s[:, j % 2, i * P:(i + 1) * P], w_out[:],
                                    start=False, stop=True, skip_group_check=True)
                last.then_inc(hs_free, 1)
                tiles = load_regs(ET.PE, t_row, gi * G, G, NT - 1)
                pe.wait_ge(ohn_ready, 1)
                pe.sem_inc(ohn_ready, -1)
                if j % 2 == 1:
                    pe.sem_inc(bd_free, 1)
                for i in range(G):
                    o = b + G * D + i * D
                    for s in range(3):
                        last = t.matmul(ps[:, o:o + D], oh_n[:, j, i * P:(i + 1) * P], part3[:, s, ds(tiles[i] * D, D)],
                                        start=(s == 0), stop=(s == 2), skip_group_check=True)
                last.then_inc(wq_ready, 1)

            def scatter0(gi, j):
                pe.wait_ge(msg_ready, 1)
                pe.sem_inc(msg_ready, -1)
                tiles = load_regs(ET.PE, t_row, gi * G, G, NT - 1)
                for i in range(G):
                    for s in range(3):
                        last = t.matmul(ps[:, ds(tiles[i] * D, D)], oh_b[:, j, i * P:(i + 1) * P],
                                        top_half(msg3[:, j, s, i * D:(i + 1) * D]),
                                        start=False, stop=True, skip_group_check=True)
                last.then_inc(oh_free, 1)

            pe.sem_inc(bd_free, 2)
            pe.sem_inc(hs_free, 2)
            for j in range(STEPS):
                hidden(j % 2)
                if j == 0:
                    pe.wait_ge(ohn_ready, 1)
                    pe.sem_inc(ohn_ready, -1)
                    pe.sem_inc(ohn_ready, 1)
                    zero(4)
                if j >= 1:
                    edge_weights(j - 1, j - 1)
                if j >= 3:
                    scatter0(j - 3, j - 3)
            with pe.Fori(1, NB) as it:
                for j in range(STEPS):
                    hidden(j % 2)
                    edge_weights(it * STEPS + j - 1, (j - 1) % STEPS)
                    scatter0(it * STEPS + j - 3, (j - 3) % STEPS)
            edge_weights(NG - 1, STEPS - 1)
            scatter0(NG - 3, STEPS - 3)
            scatter0(NG - 2, STEPS - 2)
            scatter0(NG - 1, STEPS - 1)

            pe.wait_ge(acc_free, 1)
            pe.sem_inc(acc_free, -1)
            pe.sem_inc(proj_free, 1)
            for layer in range(2):
                project(D if layer == 0 else P, w1x[:] if layer == 0 else w2x[:], H * C + 4)
                pe.wait_ge(parts_ready, 1)
                pe.sem_inc(parts_ready, -1)

                def select(c8, hb):
                    b = WQ + hb * BANK
                    pe.wait_ge(sel_free, 1)
                    pe.sem_inc(sel_free, -1)
                    pe.wait_ge(sel_oh, 1)
                    pe.sem_inc(sel_oh, -1)
                    pe.sem_inc(bc_free, 1)
                    tiles = load_regs(ET.PE, t_row, c8 * 8, 8, NT - 1)
                    for i in range(8):
                        terms = ps[:, b + i * H * NS:b + (i + 1) * H * NS].rearrange("p (h t) -> p h t", h=H)
                        for s in range(3):
                            t.matmul(terms[:, :, 0:NT], bc_s[:, hb, i * P:(i + 1) * P], as3[:, s, :, :],
                                     start=(s == 0), stop=(s == 2))
                        last = t.matmul(terms[:, :, NT:NS], oh_n8(hb)[:, i * P:(i + 1) * P],
                                        ad3[:, ds(tiles[i] * (H * 3), H * 3)].rearrange("p (h s) -> p h s", h=H),
                                        start=True, stop=True)
                    last.then_inc(sel_mm, 1)

                with pe.Fori(0, NB) as it:
                    for hb in range(2):
                        select(it * 2 + hb, hb)
                pe.wait_ge(sel_free, 2)
                pe.sem_inc(sel_free, -2)
                pe.wait_ge(lrow_ready, 1)
                pe.sem_inc(lrow_ready, -1)
                for h in range(H):
                    for k in range(KB):
                        last = t.transpose(ps[:, (2 * h) * BANK + k * P:(2 * h) * BANK + (k + 1) * P],
                                           l_e[:, h, k * P:(k + 1) * P], ident[:])
                    last.then_inc(lrow_mm, 1)
                for h in range(H):
                    pe.wait_ge(ends_ready, 1)
                    pe.sem_inc(ends_ready, -1)
                    columns_to_rows(carry_c[:, 0:KB], carry_c[:, KB:2 * KB]).then_inc(ends_mm, 1)
                    carries_to_columns()
                    rows_to_columns()
                    pe.wait_ge(exp_ready, 1)
                    pe.sem_inc(exp_ready, -1)
                    for k in range(KB):
                        last = t.transpose(ps[:, k * P:(k + 1) * P], l_r[:, h, k * P:(k + 1) * P], ident[:])
                    last.then_inc(prow_mm, 1)
                pe.wait_ge(acc_free, 1)
                pe.sem_inc(acc_free, -1)
                zero(7)

                with pe.Fori(0, NB) as it:
                    for j in range(STEPS):
                        pe.wait_ge(msg_ready, 1)
                        pe.sem_inc(msg_ready, -1)
                        pe.sem_inc(ring_free, 1)
                        at = it * BODY + j * G
                        tiles = load_regs(ET.PE, t_row, at, G, NT - 1)
                        for i in range(G):
                            o = i * P
                            t.matmul(ps[:, ds(tiles[i] * P, P)], oh_e[:, j, o:o + P], msg[:, j, o:o + P],
                                     start=False, stop=True, skip_group_check=True)
                            last = t.matmul(ps[:, ds(tiles[i] * NX + SUMS, NX)], oh_e[:, j, o:o + P],
                                            ex[:, :, ds(at + i, 1)], start=False, stop=True, skip_group_check=True)
                        last.then_inc(oh_free, 1)
                pe.wait_ge(acc_free, 1)
                pe.sem_inc(acc_free, -1)


N_WEIGHTS = 23


def kernel(**inputs):
    import numpy as np
    import concourse.bacc as bacc
    from concourse.bass_utils import run_bass_kernel_spmd as run

    def rows(a, pad):
        full = np.full((NIP * P,), pad, a.dtype)
        full[:E] = a
        return full.reshape(NIP, P)

    a = {k: np.ascontiguousarray(v) for k, v in inputs.items()}
    attrs = np.zeros((F, EP), a["edge_attr_8"].dtype)
    attrs[:F8, :E] = a["edge_attr_8"].T
    attrs[F8:, :E] = a["edge_attr_16"].T
    arrays = {"x": a["x"], "src_rows": rows(a["src"], 0), "dst_rows": rows(a["dst"], DST_PAD),
              "ew_rows": rows(a["edge_weight"], 0), "attrs": attrs}
    for k in ("W_rad1", "b_rad1", "W_rad2", "b_rad2", "W_sph1", "b_sph1", "W_sph2", "b_sph2", "Wq", "Wk", "Wv"):
        arrays[k] = a["L0_gnn_" + k]
    for k in ("W1", "as1", "ad1", "b1", "W2", "as2", "ad2", "b2"):
        arrays[k] = a["L1_gnn_" + k]
    nc = bacc.Bacc("TRN2", target_bir_lowering=False, num_devices=1)
    args = [nc.dram_tensor(k, v.shape, mybir.dt.from_np(v.dtype), kind="ExternalInput").ap() for k, v in arrays.items()]
    out = nc.dram_tensor("out", (N, D), mybir.dt.float32, kind="ExternalOutput").ap()
    gnn(nc, *args, out)
    r = run(nc, [arrays], core_ids=[0])
    return r.results[0]["out"]
```

```python
import concourse.bass as bass
from concourse import mybir
from concourse.alu_op_type import AluOpType as ALU
from contextlib import ExitStack

P = 128
N, D, E = 3125, 64, 103125
NT = -(-N // P)
TAIL = N - (NT - 1) * P
NCH = -(-E // P)
G = 4
STEPS = 4
BODY = G * STEPS
NI = -(-(NCH + NT - 1) // BODY) * BODY
NB = NI // BODY
KB = -(-NI // P)
NIP = KB * P
NG = NI // G
RING = 9 * BODY
RG = RING // G
RB = RG // STEPS
TURNS = NI // RING
REST = NI % RING
F8, F16 = 8, 16
F = F8 + F16
EP = NIP * P
DST_PAD = 4095
HEADS, HD = 8, 8
NX = 5
H, C = 2, 64
AVG = 32.0
EPS = 1e-5
BIG = 2.0 ** 100
BANK = 512
TG = 5
A_AT = (32, 64, 96)
PA = A_AT[2] + F
PL = 65
NS = NT + 3


def gnn(nc, x, src_rows, dst_rows, ew_rows, attrs, w_rad1, b_rad1, w_rad2, b_rad2, w_sph1, b_sph1, w_sph2, b_sph2,
        wq, wk, wv, g1_w, g1_as, g1_ad, g1_b, g2_w, g2_as, g2_ad, g2_b, out):
    f32, bf16, i32 = mybir.dt.float32, mybir.dt.bfloat16, mybir.dt.int32
    ACT = mybir.ActivationFunctionType
    AX = mybir.AxisListType
    ET = mybir.EngineType
    ds = bass.ds
    ctx = ExitStack()
    with ctx:
        def sb(name, shape, dt=f32):
            return ctx.enter_context(nc.sbuf_tensor(name, shape, dt))

        def sem(name):
            return ctx.enter_context(nc.semaphore(name))

        table = nc.dram_tensor("table", [NT * P, P], f32, kind="Internal").ap()
        ds_dram = nc.dram_tensor("ds_dram", [NIP // 8, 2, 8 * P], bf16, kind="Internal").ap()

        iota_f = sb("iota_f", [P, P])
        iota_p = sb("iota_p", [P, 1])
        minus_p = sb("minus_p", [P, 1])
        iota_t = sb("iota_t", [P, NT])
        tile_no = sb("tile_no", [P, NT - 1])
        item_no = sb("item_no", [P, KB])
        ident = sb("ident", [P, P])
        ones = sb("ones", [P, P])
        ones_bf = sb("ones_bf", [PL, P], bf16)
        iota_b = sb("iota_b", [P, P], bf16)
        zeros_bf = sb("zeros_bf", [1, BANK], bf16)
        w_in = sb("w_in", [PA, P])
        w_in3 = sb("w_in3", [PA, 3, P], bf16)
        b_in = sb("b_in", [P, 1])
        w_out = sb("w_out", [P, D])
        b_out2 = sb("b_out2", [PL, 2, D])
        b_part = sb("b_part", [PL, 3, D])
        b_out = sb("b_out", [PL, G, D], bf16)
        w_qkv = sb("w_qkv", [D, 3 * D])
        w1x = sb("w1x", [D, H * C + 4])
        w2x = sb("w2x", [P, H * C + 4])
        att = sb("att", [P, 4, H * C])
        b1_b = sb("b1_b", [P, H * C])
        b2_b = sb("b2_b", [P, C])
        x1 = sb("x1", [P, NT * D])
        h_in = sb("h_in", [P, NT * H * C])
        stat = sb("stat", [P, 4, NT])
        node_m = sb("node_m", [P, 6, NT * H])
        part3 = h_in[:, 0:3 * NT * D // 2].bitcast(bf16).rearrange("p (s n) -> p s n", s=3)
        asd = sb("asd", [P, NT, 4])
        res = sb("res", [P, 2, NT * 4])
        as3 = sb("as3", [P, 3, H, NT], bf16)
        ad3 = sb("ad3", [P, NT * H * 3], bf16)
        stage_xT = sb("stage_xT", [P, 2 * TG * P])
        stage, xT = stage_xT[:, 0:TG * P], stage_xT[:, TG * P:2 * TG * P]
        attrs_t = stage_xT[0:PA, 0:2 * G * P].rearrange("p (b n) -> p b n", b=2)
        last_i = sb("last_i", [P, KB], i32)
        last_f = sb("last_f", [P, KB])
        cmp_a = sb("cmp_a", [P, KB * (NT - 1)])
        cnt = sb("cnt", [P, NT - 1])
        first_item = sb("first_item", [P, NT - 1])
        t_col = sb("t_col", [P, KB])
        t128 = sb("t128", [P, KB])
        c_col = sb("c_col", [P, KB])
        c_idx = sb("c_idx", [P, KB], i32)
        t_row = sb("t_row", [1, NIP], i32)
        c_row = sb("c_row", [1, NIP], i32)
        tmp_r = sb("tmp_r", [P, KB, P])
        src_e = sb("src_e", [P, NIP], i32)
        idx = sb("idx", [P, RING], i32)
        dl_e = sb("dl_e", [P, NIP])
        hi_e = sb("hi_e", [P, NIP], bf16)
        ew_e = sb("ew_e", [P, NIP])
        keep_f = sb("keep_f", [P, KB, P], bf16)
        keep_b = sb("keep_b", [P, KB, P], bf16)
        not_first = sb("not_first", [P, KB, P], bf16)
        not_last = sb("not_last", [P, KB, P], bf16)
        links = sb("links", [1, 4, NIP], bf16)
        carry_c = sb("carry_c", [P, 2 * KB])
        carry_k = sb("carry_k", [P, 2 * KB])
        edge_x = sb("edge_x", [P, (H + NX) * NIP])
        l_r = edge_x[:, 0:H * NIP].rearrange("p (h n) -> p h n", h=H)
        ex = edge_x[:, H * NIP:(H + NX) * NIP].rearrange("p (q n) -> p q n", q=NX)
        p_e, l_e, ind_e = ex[:, 0:H, :], ex[:, H:2 * H, :], ex[:, 2 * H, :]
        t_a = edge_x[:, 2 * H * NIP:2 * H * NIP + NT * D]
        kv_rows = edge_x[:, 0:NT * P].rearrange("p (t f) -> p t f", f=P)
        ring = sb("ring", [P, RING, P])
        attrs_b = sb("attrs_b", [PA, 2, G * P], bf16)
        bc_d = sb("bc_d", [P, 2, 8 * P], bf16)
        bc_s = sb("bc_s", [P, 2, 8 * P], bf16)
        hid_s = bc_s[:].rearrange("p a n -> p (a n)").bitcast(f32).rearrange("p (a n) -> p a n", a=2)
        oh_n = sb("oh_n", [P, 4, G * P], bf16)
        work = sb("work", [P, 2 * STEPS, G * P])
        oh_e, msg = work[:, 0:STEPS, :], work[:, STEPS:2 * STEPS, :]
        oh_b = work[:, 0:STEPS // 2, :].rearrange("p a n -> p (a n)").bitcast(bf16).rearrange("p (j n) -> p j n", j=STEPS)
        msg3 = work[:, STEPS // 2:2 * STEPS, :].rearrange("p a n -> p (a n)").rearrange("p (j s n) -> p j s n", j=STEPS, s=3)
        top_half = lambda t: t.bitcast(bf16)[:, 1::2]
        bc_ds = work[:].rearrange("p a n -> p (a n)").bitcast(bf16).rearrange("p (b n) -> p b n", b=4)
        blk = lambda n: work[:, 2 * n:2 * n + 2, :].rearrange("p a n -> p (a n)")[:, 0:KB * P].rearrange("p (k e) -> p k e", e=P)
        src_r, dst_ri, ew_r, tmp_i = blk(0).bitcast(i32), blk(1).bitcast(i32), blk(2), blk(3).bitcast(i32)
        bf_r = [bc_s[:, n, 0:KB * P] for n in range(2)]
        dst_r = oh_n[:].rearrange("p a n -> p (a n)").bitcast(f32)[:, 0:NIP].rearrange("p (k e) -> p k e", e=P)
        w_rows = work[0:1].rearrange("p a n -> p (a n)")
        ends, runs = (w_rows[:, n * NIP:(n + 2) * NIP].rearrange("p (a n) -> p a n", a=2) for n in (0, 2))
        oh_hi = sb("oh_hi", [P, 2, 8 * NS], bf16)
        t12 = sb("t12", [P, 2 * G * D])
        w_rest = t12[0:PA, 0:2 * P].rearrange("p (s n) -> p s n", s=2)
        att_prod = t12[:, 2 * P:2 * P + H * C]
        t1, t2 = t12[:, 0:G * D], t12[:, G * D:2 * G * D]
        sel = [t12[:, 0:8 * H * NS], stage[:, 0:8 * H * NS]]
        first_act = sb("first_act", [1, 1])
        al = sb("al", [P, G * HEADS])
        alw = sb("alw", [P, G * HEADS])

        oh_n8 = lambda b: oh_n[:, 2 * b:2 * b + 2, :].rearrange("p a n -> p (a n)")
        hi8 = lambda b: oh_hi[:, b, :].rearrange("p (g t) -> p g t", t=NS)
        h_rows = h_in[:].rearrange("p (t f) -> p t f", f=P)

        ps = ctx.enter_context(nc.psum_tensor("ps", [P, 8 * BANK], f32))
        HID = 4 * BANK
        WQ = 6 * BANK
        SUMS = 6 * BANK + NT * H * C - 6 * BANK
        MAX_AT, EXP_AT, CARRY = 4 * BANK, 6 * BANK, 8 * BANK - 2 * KB
        by_row = lambda t: t.rearrange("p (k e) -> p k e", e=P)
        assert EXP_AT + NIP <= CARRY
        assert SUMS + NT * NX <= 7 * BANK

        consts_made = sem("consts_made")
        consts_f = sem("consts_f")
        weights_in = sem("weights_in")
        x_in = sem("x_in")
        last_in = sem("last_in")
        cnt_ready = sem("cnt_ready")
        cs_ready = sem("cs_ready")
        cidx_ready = sem("cidx_ready")
        tc_ready = sem("tc_ready")
        tcrow_mm = sem("tcrow_mm")
        rows_t = sem("rows_t")
        rows_gathered = sem("rows_gathered")
        bfrow_ready = sem("bfrow_ready")
        bfrow_out = sem("bfrow_out")
        tr_ready = sem("tr_ready")
        tr_mm = sem("tr_mm")
        tr_done = sem("tr_done")
        items_ready = sem("items_ready")
        chain = sem("chain")
        achain = sem("achain")
        in_ready = sem("in_ready")
        stage_ready = sem("stage_ready")
        stage_mm = sem("stage_mm")
        xT_ready = sem("xT_ready")
        proj_mm = sem("proj_mm")
        proj_free = sem("proj_free")
        rows_ready = sem("rows_ready")
        rows_written = sem("rows_written")
        proj_done = sem("proj_done")
        parts_ready = sem("parts_ready")
        idx_staged = sem("idx_staged")
        g_sem = [sem(f"g_sem{i}") for i in range(4)]
        gathered = sem("gathered")
        ring_free = sem("ring_free")
        at_ready = [sem(f"at_ready{i}") for i in range(2)]
        at_free = sem("at_free")
        bd_ready = [sem(f"bd_ready{i}") for i in range(2)]
        bd_free = sem("bd_free")
        chain_a = sem("chain_a")
        parts_a = sem("parts_a")
        ab_ready = sem("ab_ready")
        bc_ready = [sem(f"bc_ready{i}") for i in range(4)]
        bc_free = sem("bc_free")
        hi_made = sem("hi_made")
        chain_s = sem("chain_s")
        hid_mm = sem("hid_mm")
        hs_ready = sem("hs_ready")
        hs_free = sem("hs_free")
        ohn_ready = sem("ohn_ready")
        wq_ready = sem("wq_ready")
        wq_free = sem("wq_free")
        msg_ready = sem("msg_ready")
        oh_free = sem("oh_free")
        sel_oh = sem("sel_oh")
        sel_mm = sem("sel_mm")
        sel_free = sem("sel_free")
        lrow_ready = sem("lrow_ready")
        lrow_mm = sem("lrow_mm")
        ends_ready = sem("ends_ready")
        ends_mm = sem("ends_mm")
        carry_ready = sem("carry_ready")
        carry_mm = sem("carry_mm")
        shift_ready = sem("shift_ready")
        exp_ready = sem("exp_ready")
        prow_mm = sem("prow_mm")
        exp_out = sem("exp_out")
        exp_nodes = sem("exp_nodes")
        acc_free = sem("acc_free")
        var_ready = sem("var_ready")
        sd_ready = sem("sd_ready")
        out_ready = sem("out_ready")
        out_done = sem("out_done")

        def load_regs(engine, row, at, n, top):
            _, v = nc.values_load_multi_w_load_instructions(
                row[0:1, ds(at, n)], engines=[engine], min_val=0, max_val=top,
                skip_runtime_bounds_check_because="worked out as a count of at most that many")
            return v

        block = ctx.enter_context(nc.Block())

        @block.sync
        def _(sp):
            sp.dma_start(last_i[:], dst_rows.rearrange("(k p) e -> p k e", p=P)[:, :, P - 1],
                         allow_slow_non_contiguous=True).then_inc(last_in, 16)
            sp.dma_start(x1[:, 0:(NT - 1) * D].rearrange("p (t d) -> p t d", d=D),
                         x[0:(NT - 1) * P, :].rearrange("(t p) d -> p t d", p=P)).then_inc(x_in, 16)
            sp.wait_ge(consts_f, 1)
            sp.dma_start(x1[0:TAIL, (NT - 1) * D:NT * D], x[(NT - 1) * P:N, :]).then_inc(x_in, 16)
            n = 0
            for dst, s in (*((w_in[r:r + F8, 0:D], w_rad1) for r in A_AT),
                           *((w_in[r + F8:r + F, D:2 * D], w_sph1) for r in A_AT),
                           (b_in[0:D, :], b_rad1.rearrange("(d a) -> d a", a=1)),
                           (b_in[D:P, :], b_sph1.rearrange("(d a) -> d a", a=1)),
                           (w_out[0:D, :], w_rad2), (w_out[D:P, :], w_sph2),
                           *((b_out2[32 * s:32 * s + 1, i, :], b.rearrange("(a d) -> a d", a=1))
                             for s in range(3) for i, b in enumerate((b_rad2, b_sph2))),
                           (w_qkv[:, 0:D], wq), (w_qkv[:, D:2 * D], wk), (w_qkv[:, 2 * D:3 * D], wv),
                           (w1x[:, 0:H * C], g1_w), (w2x[:, 0:H * C], g2_w),
                           (att[:, 0, :], g1_as.rearrange("h c -> (h c)").partition_broadcast(P)),
                           (att[:, 1, :], g1_ad.rearrange("h c -> (h c)").partition_broadcast(P)),
                           (att[:, 2, :], g2_as.rearrange("h c -> (h c)").partition_broadcast(P)),
                           (att[:, 3, :], g2_ad.rearrange("h c -> (h c)").partition_broadcast(P)),
                           (b1_b[:], g1_b.partition_broadcast(P)), (b2_b[:], g2_b.partition_broadcast(P))):
                sp.dma_start(dst, s).then_inc(weights_in, 16)
                n += 1
            assert n == N_WEIGHTS
            sp.wait_ge(bfrow_ready, 1)
            sp.sem_inc(bfrow_ready, -1)
            for k in range(KB):
                for s in range(2):
                    sp.dma_start(ds_dram[k * P // 8:(k + 1) * P // 8, s, :].rearrange("a (b e) -> a b e", e=P),
                                 bf_r[s][:, k * P:(k + 1) * P]).then_inc(bfrow_out, 16)

            def write_table(row_out):
                with sp.Fori(0, NT // TG) as i:
                    sp.wait_ge(rows_ready, 1)
                    sp.sem_inc(rows_ready, -1)
                    sp.dma_start(table.rearrange("(t p) f -> p t f", p=P)[:, ds(i * TG, TG), :],
                                 row_out[:, ds(i * TG, TG), :]).then_inc(rows_written, 16)

            def load_attrs(gb, chunks):
                sp.wait_ge(at_free, 1)
                sp.sem_inc(at_free, -1)
                for j in range(G):
                    sp.dma_start(attrs_t[A_AT[0]:PA, gb, j * P:(j + 1) * P], attrs[:, ds(chunks[j] * P, P)]
                                 ).then_inc(at_ready[gb], 16)

            write_table(kv_rows)
            sp.wait_ge(bfrow_out, 16 * 2 * KB)
            sp.wait_ge(items_ready, 1)
            sp.sem_inc(items_ready, -1)
            with sp.Fori(0, NB) as it:
                for hb in range(2):
                    sp.wait_ge(bd_free, 1)
                    sp.sem_inc(bd_free, -1)
                    sp.dma_start(bc_d[:, hb, :], ds_dram[ds(it * 2 + hb, 1), 0, :].rearrange("a e -> (a e)")
                                 .partition_broadcast(P)).then_inc(bd_ready[hb], 16)
                    cs = load_regs(ET.SP, c_row, it * BODY + hb * 8, 8, NIP - 1)
                    for gb in range(2):
                        load_attrs(gb, cs[gb * G:gb * G + G])
            load_attrs(0, load_regs(ET.SP, c_row, NI, G, NIP - 1))
            for layer in range(2):
                write_table(h_rows)
                with sp.Fori(0, NI // 32) as it:
                    for b in range(4):
                        sp.wait_ge(bc_free, 1)
                        sp.sem_inc(bc_free, -1)
                        sp.dma_start(bc_ds[:, b, :], ds_dram[ds(it * 4 + b, 1), :, :].rearrange("a s e -> (a s e)")
                                     .partition_broadcast(P)).then_inc(bc_ready[b], 16)
            sp.wait_ge(out_ready, 1)
            sp.sem_inc(out_ready, -1)
            sp.dma_start(out[0:(NT - 1) * P, :].rearrange("(t p) d -> p t d", p=P),
                         t_a[:, 0:(NT - 1) * D].rearrange("p (t d) -> p t d", d=D)).then_inc(out_done, 16)
            sp.dma_start(out[(NT - 1) * P:N, :], t_a[0:TAIL, (NT - 1) * D:NT * D]).then_inc(out_done, 16)
            sp.wait_ge(out_done, 32)

        @block.gpsimd
        def _(pool):
            g = nc.gpsimd
            g.iota(iota_f[:], [[1, P]], base=0, channel_multiplier=0, allow_small_or_imprecise_dtypes=True)
            g.iota(iota_p[:], [[1, 1]], base=0, channel_multiplier=1, allow_small_or_imprecise_dtypes=True)
            g.iota(iota_t[:], [[1, NT]], base=0, channel_multiplier=0, allow_small_or_imprecise_dtypes=True)
            g.iota(tile_no[:], [[1, NT - 1]], base=1, channel_multiplier=0, allow_small_or_imprecise_dtypes=True)
            g.iota(item_no[:], [[P, KB]], base=0, channel_multiplier=1,
                   allow_small_or_imprecise_dtypes=True).then_inc(consts_made, 1)
            pool.wait_ge(cidx_ready, 1)
            pool.sem_inc(cidx_ready, -1)
            for k in range(KB):
                for dst, rows in ((dst_ri, dst_rows), (src_r, src_rows), (ew_r, ew_rows)):
                    g.indirect_dma_start(dst[:, k, :], None, rows, bass.IndirectOffsetOnAxis(c_idx[:, k:k + 1], 0)
                                         ).then_inc(rows_gathered, 16)
            pool.sem_inc(ring_free, RG)
            pool.wait_ge(rows_t, 1)

            def pass_on(layer, turn, q):
                pool.wait_ge(g_sem[q % 4], layer * (16 * G * NG // 4) + turn * (16 * G * RG // 4) + 16 * G * (q // 4 + 1))
                pool.sem_inc(gathered, 1)

            def gather_turn(layer, turn, slots):
                for q in range(slots // G):
                    if q % 4 == 0:
                        s0 = q * G
                        g.tensor_copy(idx[:, s0:s0 + BODY], src_e[:, ds(turn * RING + s0, BODY)]
                                      ).then_inc(idx_staged, 1)
                        pool.wait_ge(idx_staged, 1)
                        pool.sem_inc(idx_staged, -1)
                    pool.wait_ge(ring_free, 1)
                    pool.sem_inc(ring_free, -1)
                    for j in range(G):
                        s = q * G + j
                        g.indirect_dma_start(ring[:, s, :], None, table, bass.IndirectOffsetOnAxis(idx[:, s:s + 1], 0)
                                             ).then_inc(g_sem[q % 4], 16)
                    if q >= 3:
                        pass_on(layer, turn, q - 3)
                for q in range(slots // G - 3, slots // G):
                    pass_on(layer, turn, q)

            with pool.Fori(0, 3) as layer:
                pool.wait_ge(rows_written, 16 * (NT // TG))
                pool.sem_inc(rows_written, -(16 * (NT // TG)))
                with pool.Fori(0, TURNS) as turn:
                    gather_turn(layer, turn, RING)
                gather_turn(layer, TURNS, REST)

        @block.scalar
        def _(act):
            a = nc.scalar

            def evacuate(width, row_out, first, n_side, side):
                a.copy(first_act[:], ones[0:1, 0:1]).then_inc(achain, 1)
                act.wait_ge(achain, 1)
                act.sem_inc(achain, -1)
                with act.Fori(0, NT // TG) as i:
                    act.wait_ge(stage_mm, 1)
                    act.sem_inc(stage_mm, -1)
                    a.copy(xT[0:width, :], ps[0:width, 0:TG * P]).then_inc(xT_ready, 1)
                    act.wait_ge(proj_mm, 1)
                    act.sem_inc(proj_mm, -1)
                    pr = ps[:, 2 * BANK:2 * BANK + TG * 256].rearrange("p (t f) -> p t f", f=256)
                    a.copy(row_out[:, ds(i * TG, TG), :], pr[:, :, first:first + P]).then_inc(rows_ready, 1)
                    o = 0 if first else P
                    a.copy(side[:, ds(i * TG * n_side, TG * n_side)].rearrange("p (t f) -> p t f", f=n_side),
                           pr[:, :, o:o + n_side]).then_inc(proj_free, 1)
                act.drain().then_inc(proj_done, 1)

            def sqrt_var():
                act.wait_ge(var_ready, 1)
                act.sem_inc(var_ready, -1)
                a.activation(stat[:, 2, :], stat[:, 1, :], ACT.Sqrt).then_inc(sd_ready, 1)

            act.wait_ge(consts_f, 1)
            evacuate(D, kv_rows, D, D, t_a)

            def silu(gb):
                act.wait_ge(hid_mm, 1)
                act.sem_inc(hid_mm, -1)
                act.sem_inc(at_free, 1)
                act.wait_ge(hs_free, 1)
                act.sem_inc(hs_free, -1)
                a.activation(hid_s[:, gb, :], ps[:, HID + gb * BANK:HID + (gb + 1) * BANK], ACT.Silu,
                             bias=b_in[:, 0:1]).then_inc(hs_ready, 1)

            def pack_attrs(gb):
                act.wait_ge(parts_a, 1)
                act.sem_inc(parts_a, -1)
                a.copy(attrs_b[:, gb, :], top_half(attrs_t[0:PA, gb, :])).then_inc(ab_ready, 1)

            act.wait_ge(weights_in, 16 * N_WEIGHTS)
            act.sem_inc(at_free, 2)
            a.activation(first_act[:], b_in[0:1, 0:1], ACT.Silu).then_inc(achain, 1)
            act.wait_ge(achain, 1)
            act.sem_inc(achain, -1)

            def one_hot_nodes(j):
                if j % 2 == 0:
                    act.wait_ge(bd_ready[j // 2], 16)
                    act.sem_inc(bd_ready[j // 2], -16)
                d = bc_d[:, j // 2, (j % 2) * G * P:(j % 2 + 1) * G * P]
                a.activation(d, d, ACT.Abs, bias=minus_p[:, 0:1]).then_inc(achain, 1)
                act.wait_ge(achain, 1)
                act.sem_inc(achain, -1)
                a.activation(oh_n[:, j, :], d, ACT.Relu, bias=ones[:, 0:1], scale=-1.0).then_inc(ohn_ready, 1)

            pack_attrs(0)
            one_hot_nodes(0)
            one_hot_nodes(1)

            def body0(ahead):
                for j in range(STEPS):
                    silu(j % 2)
                    pack_attrs(1 - j % 2)
                    if j < ahead:
                        one_hot_nodes((j + 2) % STEPS)

            with act.Fori(0, NB - 1) as it:
                body0(STEPS)
            body0(STEPS - 2)
            sqrt_var()
            for layer in range(2):
                evacuate(D if layer == 0 else P, h_rows, 0, 4, asd[:, :, :].rearrange("p t f -> p (t f)"))
                for h in range(H):
                    act.wait_ge(shift_ready, 1)
                    act.sem_inc(shift_ready, -1)
                    a.activation(l_r[:, h, :], l_r[:, h, :], ACT.Exp).then_inc(exp_ready, 1)
                act.wait_ge(shift_ready, 1)
                act.sem_inc(shift_ready, -1)
                a.activation(node_m[:, 4:6, :], node_m[:, 2:4, :], ACT.Exp).then_inc(exp_nodes, 1)
            sqrt_var()

        @block.vector
        def _(dve):
            v = nc.vector

            def link(ins, n=1):
                ins.then_inc(chain, 1)
                dve.wait_ge(chain, 1)
                dve.sem_inc(chain, -1)

            v.memset(x1[:, (NT - 1) * D:NT * D], 0.0)
            v.memset(w_in[:], 0.0)
            v.memset(attrs_t[:], 0.0)
            v.memset(b_out[:], 0.0)
            v.memset(b_out2[:], 0.0)
            v.memset(oh_hi[:], 1.0)
            v.memset(ones[:], 1.0)
            v.memset(ones_bf[:], 1.0)
            v.memset(zeros_bf[:], 0.0)
            v.memset(links[:], -BIG)
            v.memset(keep_f[:], -BIG)
            v.memset(keep_b[:], -BIG).then_inc(consts_f, 1)
            dve.wait_ge(consts_f, 1)
            dve.wait_ge(consts_made, 1)
            v.tensor_copy(iota_b[:], iota_f[:])
            v.tensor_scalar(minus_p[:], iota_p[:], -1.0, None, ALU.mult)
            link(v.tensor_scalar(ident[:], iota_f[:], iota_p[:, 0:1], None, ALU.is_equal))
            dve.wait_ge(last_in, 16)
            link(v.tensor_copy(last_f[:], last_i[:]))
            ca = cmp_a[:].rearrange("p (t k) -> p t k", k=KB)
            link(v.tensor_scalar(cnt[:], tile_no[:], float(P), None, ALU.mult))
            link(v.tensor_tensor(ca, last_f[:].unsqueeze(1).to_broadcast([P, NT - 1, KB]),
                                 cnt[:].unsqueeze(2).to_broadcast([P, NT - 1, KB]), ALU.is_lt))
            v.tensor_reduce(cnt[:], ca, AX.X, ALU.add).then_inc(cnt_ready, 1)
            dve.wait_ge(cs_ready, 1)
            dve.sem_inc(cs_ready, -1)
            link(v.tensor_tensor(first_item[:], ps[:, 0:NT - 1], tile_no[:], ALU.add))
            cb = cmp_a[:].rearrange("p (k t) -> p k t", k=KB)
            link(v.tensor_tensor(cb, first_item[:].unsqueeze(1).to_broadcast([P, KB, NT - 1]),
                                 item_no[:].unsqueeze(2).to_broadcast([P, KB, NT - 1]), ALU.is_le))
            link(v.tensor_reduce(t_col[:], cb, AX.X, ALU.add))
            link(v.tensor_tensor(c_col[:], item_no[:], t_col[:], ALU.subtract))
            v.tensor_copy(c_idx[:], c_col[:]).then_inc(cidx_ready, 1)
            v.tensor_scalar(t128[:], t_col[:], float(P), None, ALU.mult).then_inc(tc_ready, 1)
            dve.wait_ge(tcrow_mm, 1)
            dve.sem_inc(tcrow_mm, -1)
            v.tensor_copy(t_row[:], ps[0:1, 0:NIP])
            v.tensor_copy(c_row[:], ps[0:1, 2 * BANK:2 * BANK + NIP]).then_inc(tr_done, 1)
            dve.wait_ge(weights_in, 16 * N_WEIGHTS)
            link(v.tensor_tensor(w_rest[:, 0, :], w_in[:], top_half(w_in[:]), ALU.subtract))
            link(v.tensor_tensor(w_rest[:, 1, :], w_rest[:, 0, :], top_half(w_rest[:, 0, :]), ALU.subtract))
            for s, w in enumerate((w_in[:], w_rest[:, 0, :], w_rest[:, 1, :])):
                v.tensor_copy(w_in3[:, s, :], top_half(w))
            link(v.tensor_tensor(b_part[:, 0, :], b_out2[:, 0, :], b_out2[:, 1, :], ALU.add))
            for s in range(2):
                link(v.tensor_tensor(b_part[:, s + 1, :], b_part[:, s, :], top_half(b_part[:, s, :]), ALU.subtract))
            for s in range(3):
                v.tensor_copy(b_out[32 * s:32 * s + 1, :, :],
                              top_half(b_part[32 * s:32 * s + 1, s, :]).unsqueeze(1).to_broadcast([1, G, D]))
            for wx, np_, first in ((w1x, D, 0), (w2x, P, 2)):
                for s in range(2):
                    link(v.tensor_tensor(att_prod[0:np_, :], wx[:, 0:H * C], att[0:np_, first + s, :], ALU.mult))
                    link(v.tensor_reduce(wx[:, H * C + 2 * s:H * C + 2 * s + 2],
                                         att_prod[0:np_, :].rearrange("p (h c) -> p h c", c=C), AX.X, ALU.add))

            def stage_tiles(inp, width):
                with dve.Fori(0, NT // TG) as i:
                    dve.wait_ge(in_ready, 1)
                    dve.sem_inc(in_ready, -1)
                    v.tensor_copy(stage[:, 0:TG * width], inp[:, ds(i * TG * width, TG * width)]
                                  ).then_inc(stage_ready, 1)

            dve.wait_ge(x_in, 32)
            dve.sem_inc(in_ready, 1)
            stage_tiles(x1, D)
            dve.wait_ge(proj_done, 1)
            dve.sem_inc(proj_done, -1)

            def split3(srcv, dst3, r0, r1):
                link(v.tensor_copy(dst3[0], srcv))
                link(v.tensor_tensor(r0, srcv, dst3[0], ALU.subtract))
                link(v.tensor_copy(dst3[1], r0))
                link(v.tensor_tensor(r1, r0, dst3[1], ALU.subtract))
                return v.tensor_copy(dst3[2], r1)

            hf = NT * D // 2
            for a0 in (0, hf):
                link(split3(t_a[:, a0:a0 + hf], [part3[:, s, a0:a0 + hf] for s in range(3)],
                            h_in[:, 3 * hf:4 * hf], tmp_r[:].rearrange("p k e -> p (k e)")[:, 0:hf]))

            dve.wait_ge(rows_gathered, 16 * 3 * KB)
            link(v.tensor_copy(dst_r[:], dst_ri[:]))
            for k in range(KB):
                last = v.tensor_scalar(tmp_r[:, k, :], dst_r[:, k, :], t128[:, k:k + 1], None, ALU.subtract)
            link(last)
            v.tensor_scalar(bf_r[0], tmp_r[:].rearrange("p k e -> p (k e)"), -1.0, float(P), ALU.max, ALU.min)
            link(v.tensor_scalar(tmp_i[:], src_r[:], P - 1, None, ALU.bitwise_and))
            v.tensor_copy(bf_r[1], tmp_i[:].rearrange("p k e -> p (k e)")).then_inc(bfrow_ready, 1)

            def to_edges(dst):
                dve.sem_inc(tr_ready, 1)
                dve.wait_ge(tr_mm, 1)
                dve.sem_inc(tr_mm, -1)
                return v.tensor_copy(dst, ps[:, 2 * BANK:2 * BANK + NIP])

            link(to_edges(dl_e[:]))
            link(v.tensor_copy(tmp_r[:], src_r[:]))
            to_edges(src_e[:]).then_inc(rows_t, 1)
            link(v.tensor_scalar(tmp_i[:], src_r[:], 7, None, ALU.logical_shift_right))
            link(v.tensor_copy(tmp_r[:], tmp_i[:]))
            link(to_edges(hi_e[:]))
            link(v.tensor_scalar(tmp_r[:], ew_r[:], 1.0 / (AVG * HD ** 0.5), None, ALU.mult))
            link(to_edges(ew_e[:]))

            def mask(dst, a_, b_):
                link(v.tensor_tensor(dst, a_, b_, ALU.not_equal))
                link(v.tensor_scalar(dst, dst, -BIG, None, ALU.mult))

            mask(keep_f[:, :, 1:P], dst_r[:, :, 1:P], dst_r[:, :, 0:P - 1])
            mask(keep_b[:, :, 0:P - 1], dst_r[:, :, 1:P], dst_r[:, :, 0:P - 1])
            for k in range(KB):
                v.tensor_scalar(not_first[:, k, :], dst_r[:, k, :], dst_r[:, k, 0:1], -BIG, ALU.not_equal, ALU.mult)
                last = v.tensor_scalar(not_last[:, k, :], dst_r[:, k, :], dst_r[:, k, P - 1:P], -BIG,
                                       ALU.not_equal, ALU.mult)
            link(last)

            def to_rows(dst, a_, b_):
                v.tensor_copy(carry_c[:, 0:KB], a_)
                v.tensor_copy(carry_c[:, KB:2 * KB], b_).then_inc(ends_ready, 1)
                dve.wait_ge(ends_mm, 1)
                dve.sem_inc(ends_mm, -1)
                v.tensor_copy(dst[:, 0, :], ps[0:1, 0:NIP])
                return v.tensor_copy(dst[:, 1, :], ps[0:1, 2 * BANK:2 * BANK + NIP])

            link(to_rows(ends, dst_r[:, :, 0], dst_r[:, :, P - 1]))
            carry = ends
            e0, e1 = ends[:, 0, :], ends[:, 1, :]
            R = NIP
            link(v.tensor_tensor(runs[:, 1, 0:R - 1], t_row[:, 1:R], t_row[:, 0:R - 1], ALU.not_equal))

            def link_mask(dst, a_, b_):
                link(v.tensor_tensor(runs[:, 0, 0:R - 1], a_, b_, ALU.not_equal))
                link(v.tensor_tensor(runs[:, 0, 0:R - 1], runs[:, 0, 0:R - 1], runs[:, 1, 0:R - 1], ALU.max))
                link(v.tensor_scalar(dst, runs[:, 0, 0:R - 1], -BIG, None, ALU.mult))

            link_mask(links[:, 0, 1:R], e1[:, 0:R - 1], e1[:, 1:R])
            link_mask(links[:, 1, 0:R - 1], e0[:, 1:R], e0[:, 0:R - 1])
            link_mask(links[:, 2, 1:R], e1[:, 0:R - 1], e0[:, 1:R])
            link_mask(links[:, 3, 0:R - 1], e0[:, 1:R], e1[:, 0:R - 1])
            v.memset(ends[:, :, R - 1:R], 1.0)
            v.tensor_copy(ends[:, 0, 0:R - 1], runs[:, 0, 0:R - 1]).then_inc(carry_ready, 1)
            dve.wait_ge(carry_mm, 1)
            dve.sem_inc(carry_mm, -1)
            link(v.tensor_tensor(tmp_r[:, :, 0:P - 1], dst_r[:, :, 1:P], dst_r[:, :, 0:P - 1], ALU.not_equal))
            link(v.tensor_copy(tmp_r[:, :, P - 1], ps[:, 0:KB]))
            link(to_edges(ind_e))
            dve.sem_inc(parts_ready, 1)

            def step0(gi, slot, j, make=None, finish=True, chain_on=True,
                      attrs_too=True):
                b = WQ + (j % 2) * BANK
                jn, jp = (j + 1) % STEPS, (j - 1) % STEPS
                g3 = lambda t: t.rearrange("p (g d) -> p g d", d=D)
                rows = ring[:, ds(slot * G, G), :] if chain_on else None
                rest = lambda q: v.tensor_tensor(msg3[:, jp, q + 1, :], msg3[:, jp, q, :],
                                                 top_half(msg3[:, jp, q, :]), ALU.subtract)
                if make is not None:
                    dve.wait_ge(oh_free, 1)
                    dve.sem_inc(oh_free, -1)
                if chain_on:
                    dve.wait_ge(gathered, 1)
                    dve.sem_inc(gathered, -1)
                    dve.wait_ge(wq_ready, 1)
                    dve.sem_inc(wq_ready, -1)
                    v.tensor_tensor(g3(t1), g3(ps[:, b:b + G * D]), rows[:, :, 0:D], ALU.mult).then_inc(chain, 1)
                if finish:
                    dve.wait_ge(chain_s, 1)
                    dve.sem_inc(chain_s, -1)
                    dve.sem_inc(ring_free, 1)
                    rest(0).then_inc(chain_s, 1)
                if chain_on:
                    dve.wait_ge(chain, 1)
                    dve.sem_inc(chain, -1)
                    v.tensor_tensor(t2, ps[:, b + G * D:b + 2 * G * D], t1, ALU.mult).then_inc(chain, 1)
                if make is not None and attrs_too:
                    attr_rest(j % 2, 1, A_AT[1])
                if chain_on:
                    dve.wait_ge(chain, 1)
                    dve.sem_inc(chain, -1)
                    dve.sem_inc(wq_free, 1)
                    v.tensor_reduce(al[:], t2.rearrange("p (a c) -> p a c", c=HD), AX.X, ALU.add).then_inc(chain, 1)
                if finish:
                    dve.wait_ge(chain_s, 1)
                    dve.sem_inc(chain_s, -1)
                    rest(1).then_inc(msg_ready, 1)
                if chain_on:
                    dve.wait_ge(chain, 1)
                    dve.sem_inc(chain, -1)
                    v.tensor_tensor(alw[:].rearrange("p (g h) -> p g h", h=HEADS),
                                    al[:].rearrange("p (g h) -> p g h", h=HEADS),
                                    ew_e[:, ds(gi * G, G)].unsqueeze(2).to_broadcast([P, G, HEADS]), ALU.mult
                                    ).then_inc(chain, 1)
                if make is not None and attrs_too:
                    attr_rest(j % 2, 2, A_AT[2])
                if chain_on:
                    dve.wait_ge(chain, 1)
                    dve.sem_inc(chain, -1)
                    v.tensor_tensor(msg3[:, j, 0, :].rearrange("p (g h c) -> p g h c", g=G, c=HD),
                                    rows[:, :, D:2 * D].rearrange("p g (h c) -> p g h c", c=HD),
                                    alw[:].rearrange("p (g h) -> p g h", h=HEADS).unsqueeze(3)
                                    .to_broadcast([P, G, HEADS, HD]), ALU.mult).then_inc(chain_s, 1)
                if make is not None:
                    for i in range(G):
                        v.tensor_scalar(oh_b[:, jn, i * P:(i + 1) * P], iota_b[:],
                                        dl_e[:, ds(make * BODY + jn * G + i, 1)], None, ALU.is_equal)

            def attr_rest(gb, n, first):
                if n == 1:
                    dve.wait_ge(at_ready[gb], 16 * G)
                    dve.sem_inc(at_ready[gb], -(16 * G))
                else:
                    dve.wait_ge(chain_a, 1)
                    dve.sem_inc(chain_a, -1)
                at = attrs_t[first:PA, gb, :]
                v.tensor_tensor(at, at, top_half(at), ALU.subtract).then_inc(chain_a if n == 1 else parts_a, 1)

            for gb in range(2):
                for n in (1, 2):
                    attr_rest(gb, n, A_AT[n])
            dve.sem_inc(oh_free, STEPS)
            dve.sem_inc(wq_free, 2)
            step0(None, None, STEPS - 1, make=0, finish=False, chain_on=False, attrs_too=False)
            for j in range(1, STEPS):
                step0(j - 1, j - 1, j - 1, make=0, finish=j > 1)
            with dve.Fori(1, RB) as it:
                for j in range(STEPS):
                    step0(it * STEPS + j - 1, it * STEPS + j - 1, (j - 1) % STEPS, make=it)

            def turn0(turn, bodies):
                for j in range(STEPS):
                    it = turn * RB
                    step0(it * STEPS + j - 1, RG - 1 if j == 0 else j - 1, (j - 1) % STEPS, make=it)
                with dve.Fori(1, bodies) as r:
                    for j in range(STEPS):
                        it = turn * RB + r
                        step0(it * STEPS + j - 1, r * STEPS + j - 1, (j - 1) % STEPS, make=it)

            with dve.Fori(1, TURNS) as turn:
                turn0(turn, RB)
            turn0(TURNS, REST // BODY)
            step0(NG - 1, REST // G - 1, STEPS - 1)
            step0(None, None, 0, chain_on=False)

            def layer_norm(dst, srcv):
                s3 = lambda t: t.rearrange("p (t d) -> p t d", d=D)
                bc = lambda t: t.unsqueeze(2).to_broadcast([P, NT, D])
                link(v.tensor_reduce(stat[:, 0, :], s3(srcv), AX.X, ALU.add))
                link(v.tensor_scalar(stat[:, 0, :], stat[:, 0, :], 1.0 / D, None, ALU.mult))
                link(v.tensor_tensor(s3(srcv), s3(srcv), bc(stat[:, 0, :]), ALU.subtract))
                sq = h_in[:, 0:NT * D]
                link(v.tensor_tensor(sq, srcv, srcv, ALU.mult))
                link(v.tensor_reduce(stat[:, 1, :], s3(sq), AX.X, ALU.add))
                v.tensor_scalar(stat[:, 1, :], stat[:, 1, :], 1.0 / D, EPS, ALU.mult, ALU.add).then_inc(var_ready, 1)
                dve.wait_ge(sd_ready, 1)
                dve.sem_inc(sd_ready, -1)
                link(v.reciprocal(stat[:, 3, :], stat[:, 2, :]))
                return v.tensor_tensor(s3(dst), s3(srcv), bc(stat[:, 3, :]), ALU.mult)

            dve.wait_ge(oh_free, STEPS)
            link(v.tensor_tensor(t_a, ps[:, 0:NT * D], x1[:], ALU.add))
            dve.sem_inc(acc_free, 1)
            link(layer_norm(x1[:], t_a))

            for layer in range(2):
                dve.sem_inc(in_ready, 1)
                stage_tiles(x1 if layer == 0 else h_in, D if layer == 0 else P)
                dve.wait_ge(proj_done, 1)
                dve.sem_inc(proj_done, -1)
                n = NT * H
                r0, r1 = res[:, 0, :], res[:, 1, :]
                a_src = asd[:, :, 0:H].rearrange("p t h -> p h t")
                link(split3(a_src, [as3[:, s, :, :] for s in range(3)],
                            r0[:, 0:n].rearrange("p (h t) -> p h t", h=H), r1[:, 0:n].rearrange("p (h t) -> p h t", h=H)))
                split3(asd[:, :, H:2 * H], [ad3[:].rearrange("p (t h s) -> p s t h", h=H, s=3)[:, s] for s in range(3)],
                       r0[:, 0:n].rearrange("p (t h) -> p t h", h=H), r1[:, 0:n].rearrange("p (t h) -> p t h", h=H)
                       ).then_inc(parts_ready, 1)
                dve.sem_inc(sel_free, 2)

                def make1(b, hb):
                    dve.wait_ge(bc_ready[b], 16)
                    dve.sem_inc(bc_ready[b], -16)
                    v.tensor_scalar(oh_n8(hb), bc_ds[:, b, 0:8 * P], iota_p[:, 0:1], None, ALU.is_equal)
                    v.tensor_scalar(bc_s[:, hb, :], bc_ds[:, b, 8 * P:16 * P], iota_p[:, 0:1], None, ALU.is_equal
                                    ).then_inc(sel_oh, 1)

                def tile_hot(c8, hb):
                    v.tensor_tensor(hi8(hb)[:, :, 0:NT],
                                    hi_e[:, ds(c8 * 8, 8)].unsqueeze(2).to_broadcast([P, 8, NT]),
                                    iota_t[:].unsqueeze(1).to_broadcast([P, 8, NT]), ALU.is_equal).then_inc(hi_made, 1)

                def pick(hb):
                    o = WQ + hb * BANK
                    dve.wait_ge(hi_made, 1)
                    dve.sem_inc(hi_made, -1)
                    dve.wait_ge(sel_mm, 1)
                    dve.sem_inc(sel_mm, -1)
                    v.tensor_tensor(sel[hb].rearrange("p (g h t) -> p g h t", g=8, h=H),
                                    ps[:, o:o + 8 * H * NS].rearrange("p (g h t) -> p g h t", g=8, h=H),
                                    hi8(hb).unsqueeze(2).to_broadcast([P, 8, H, NS]), ALU.mult).then_inc(chain, 1)

                def logits(c8, hb):
                    dve.wait_ge(chain, 1)
                    dve.sem_inc(chain, -1)
                    dve.sem_inc(sel_free, 1)
                    v.tensor_reduce(l_e[:, :, ds(c8 * 8, 8)], sel[hb].rearrange("p (g h t) -> p h g t", g=8, h=H),
                                    AX.X, ALU.add)

                def step1(c8, b):
                    pick(b % 2)
                    make1(b, b % 2)
                    logits(c8, b % 2)
                    tile_hot(c8 + 2, b % 2)

                dve.sem_inc(bc_free, 4)
                for hb in range(2):
                    make1(hb, hb)
                    tile_hot(hb, hb)
                for b in range(2, 4):
                    step1(b - 2, b)
                with dve.Fori(1, NI // 32) as it:
                    for b in range(4):
                        step1(it * 4 + b - 2, b)
                for hb in range(2):
                    pick(hb)
                    logits(NI // 8 - 2 + hb, hb)
                dve.wait_ge(bc_free, 4)
                dve.sem_inc(bc_free, -4)
                link(v.memset(l_e[:, :, NI:NIP], 0.0))
                v.scalar_tensor_tensor(l_e[:], l_e[:], 0.2, l_e[:], ALU.mult, ALU.max).then_inc(lrow_ready, 1)
                for h in range(H):
                    dve.wait_ge(lrow_mm, 1)
                    dve.sem_inc(lrow_mm, -1)
                    link(v.tensor_copy(l_r[:, h, :], ps[:, 2 * h * BANK:2 * h * BANK + NIP]))
                kf, kb = (m[:].rearrange("p k e -> p (k e)") for m in (keep_f, keep_b))

                def scan_rows(h):
                    lr = l_r[:, h, :]
                    v.tensor_tensor_scan(l_e[:, h, :], kf, lr, -BIG, ALU.add, ALU.max)
                    link(v.tensor_tensor_scan(p_e[:, h, ::-1], kb[:, ::-1], lr[:, ::-1], -BIG, ALU.add, ALU.max))

                def ends_out(h):
                    v.tensor_copy(carry_c[:, 0:KB], by_row(l_e[:, h, :])[:, :, P - 1])
                    v.tensor_copy(carry_c[:, KB:2 * KB], by_row(p_e[:, h, :])[:, :, 0]).then_inc(ends_ready, 1)

                def both_sides(h):
                    link(v.tensor_tensor(l_e[:, h, :], l_e[:, h, :], p_e[:, h, :], ALU.max))

                def scan_ends():
                    dve.wait_ge(ends_mm, 1)
                    dve.sem_inc(ends_mm, -1)
                    v.tensor_copy(ends[:, 0, :], ps[0:1, 0:NIP])
                    link(v.tensor_copy(ends[:, 1, :], ps[0:1, 2 * BANK:2 * BANK + NIP]))
                    v.tensor_tensor_scan(runs[:, 0, :], links[:, 0, :], ends[:, 0, :], -BIG, ALU.add, ALU.max)
                    link(v.tensor_tensor_scan(runs[:, 1, ::-1], links[:, 1, ::-1], ends[:, 1, ::-1], -BIG,
                                              ALU.add, ALU.max))
                    v.memset(carry[:, 0, 0:1], -BIG)
                    v.memset(carry[:, 1, R - 1:R], -BIG)
                    v.tensor_tensor(carry[:, 0, 1:R], runs[:, 0, 0:R - 1], links[:, 2, 1:R], ALU.add)
                    v.tensor_tensor(carry[:, 1, 0:R - 1], runs[:, 1, 1:R], links[:, 3, 0:R - 1], ALU.add
                                    ).then_inc(carry_ready, 1)

                def shift(h):
                    dve.wait_ge(carry_mm, 1)
                    dve.sem_inc(carry_mm, -1)
                    link(v.tensor_copy(carry_k[:], ps[:, CARRY:CARRY + 2 * KB]))
                    for q, off in enumerate((not_first, not_last)):
                        for k in range(KB):
                            m_k = l_e[:, h, k * P:(k + 1) * P]
                            last = v.scalar_tensor_tensor(m_k, off[:, k, :], carry_k[:, q * KB + k:q * KB + k + 1], m_k,
                                                          ALU.add, ALU.max)
                        link(last)
                    dve.sem_inc(tr_ready, 1)
                    link(v.tensor_tensor(l_r[:, h, :], l_r[:, h, :], l_e[:, h, :], ALU.subtract))
                    dve.sem_inc(shift_ready, 1)

                def maxima_out(h):
                    dve.wait_ge(tr_mm, 1)
                    dve.sem_inc(tr_mm, -1)
                    link(v.tensor_tensor(l_e[:, h, :], ps[:, MAX_AT:MAX_AT + NIP], ind_e, ALU.mult))

                scan_rows(0)
                ends_out(0)
                scan_rows(1)
                both_sides(0)
                scan_ends()
                ends_out(1)
                shift(0)
                both_sides(1)
                scan_ends()
                maxima_out(0)
                shift(1)
                maxima_out(1)
                for h in range(H):
                    dve.wait_ge(prow_mm, 1)
                    dve.sem_inc(prow_mm, -1)
                    link(v.tensor_copy(p_e[:, h, :], ps[:, EXP_AT:EXP_AT + NIP]))
                    dve.sem_inc(exp_out, 1)
                dve.sem_inc(acc_free, 1)

                def messages(at, slot, j):
                    dve.wait_ge(oh_free, 1)
                    dve.sem_inc(oh_free, -1)
                    for i in range(G):
                        v.tensor_scalar(oh_e[:, j, i * P:(i + 1) * P], iota_f[:], dl_e[:, ds(at + i, 1)],
                                        None, ALU.is_equal)
                    dve.wait_ge(gathered, 1)
                    dve.sem_inc(gathered, -1)
                    v.tensor_tensor(msg[:, j, :].rearrange("p (g h c) -> p g h c", g=G, h=H),
                                    ring[:, ds(slot, G), :].rearrange("p g (h c) -> p g h c", h=H),
                                    p_e[:, :, ds(at, G)].rearrange("p h g -> p g h").unsqueeze(3)
                                    .to_broadcast([P, G, H, C]), ALU.mult).then_inc(msg_ready, 1)

                def turn1(turn, bodies):
                    with dve.Fori(0, bodies) as r:
                        for j in range(STEPS):
                            messages(turn * RING + r * BODY + j * G, r * BODY + j * G, j)

                with dve.Fori(0, TURNS) as turn:
                    turn1(turn, RB)
                turn1(TURNS, REST // BODY)
                th = lambda q: node_m[:, q, :].rearrange("p (t h) -> p t h", h=H)
                sums = ps[:, SUMS:SUMS + NT * NX].rearrange("p (t q) -> p t q", q=NX)
                link(v.tensor_tensor(th(0), asd[:, :, 0:H], asd[:, :, H:2 * H], ALU.add))
                link(v.scalar_tensor_tensor(th(0), th(0), 0.2, th(0), ALU.mult, ALU.max))
                dve.wait_ge(oh_free, STEPS)
                link(v.tensor_scalar(th(1), sums[:, :, 2 * H:2 * H + 1].to_broadcast([P, NT, H]), -1.0, BIG,
                                     ALU.add, ALU.mult))
                link(v.tensor_tensor(th(1), sums[:, :, H:2 * H], th(1), ALU.add))
                link(v.tensor_tensor(th(4), th(0), th(1), ALU.max))
                v.tensor_tensor(th(2), th(1), th(4), ALU.subtract)
                v.tensor_tensor(th(3), th(0), th(4), ALU.subtract).then_inc(shift_ready, 1)
                dve.wait_ge(exp_nodes, 1)
                dve.sem_inc(exp_nodes, -1)
                link(v.tensor_tensor(th(0), sums[:, :, 0:H], th(4), ALU.mult))
                link(v.tensor_tensor(th(0), th(0), th(5), ALU.add))
                link(v.reciprocal(th(1), th(0)))
                link(v.tensor_tensor(node_m[:, 2:4, :], node_m[:, 4:6, :],
                                     node_m[:, 1:2, :].to_broadcast([P, 2, NT * H]), ALU.mult))
                spread = lambda q: node_m[:, q, :].unsqueeze(2).to_broadcast([P, NT * H, C])
                ac = lambda w_: w_.rearrange("p (a c) -> p a c", c=C)
                num = edge_x[:, 0:NT * H * C]
                v.tensor_tensor(ac(num), ac(ps[:, 0:NT * H * C]), spread(2), ALU.mult)
                link(v.tensor_tensor(ac(h_in[:]), ac(h_in[:]), spread(3), ALU.mult))
                dve.sem_inc(acc_free, 1)
                link(v.tensor_tensor(h_in[:], h_in[:], num, ALU.add))
                if layer == 0:
                    hv = h_in[:].rearrange("p (t f) -> p t f", f=H * C)
                    link(v.tensor_tensor(hv, hv, b1_b[:].unsqueeze(1).to_broadcast([P, NT, H * C]), ALU.add))
            hv = h_in[:].rearrange("p (t h c) -> p t h c", h=H, c=C)
            ta = t_a.rearrange("p (t d) -> p t d", d=D)
            link(v.tensor_tensor(ta, hv[:, :, 0, :], hv[:, :, 1, :], ALU.add))
            link(v.scalar_tensor_tensor(ta, ta, 1.0 / H, b2_b[:].unsqueeze(1).to_broadcast([P, NT, D]), ALU.mult, ALU.add))
            link(v.tensor_tensor(t_a, t_a, x1[:], ALU.add))
            layer_norm(t_a, t_a).then_inc(out_ready, 1)

        @block.tensor
        def _(pe):
            t = nc.tensor
            pe.wait_ge(consts_f, 1)
            pe.wait_ge(cnt_ready, 1)
            pe.sem_inc(cnt_ready, -1)
            t.matmul(ps[:, 0:NT - 1], ones[:], cnt[:], start=True, stop=True).then_inc(cs_ready, 1)
            pe.wait_ge(tc_ready, 1)
            pe.sem_inc(tc_ready, -1)

            def columns_to_rows(a_, b_):
                for k in range(KB):
                    t.matmul(ps[0:1, k * P:(k + 1) * P], a_[:, k:k + 1], ident[:], start=True, stop=True)
                for k in range(KB):
                    last = t.matmul(ps[0:1, 2 * BANK + k * P:2 * BANK + (k + 1) * P], b_[:, k:k + 1], ident[:],
                                    start=True, stop=True)
                return last

            columns_to_rows(t_col, c_col).then_inc(tcrow_mm, 1)
            pe.wait_ge(tr_done, 1)
            pe.sem_inc(tr_done, -1)
            pe.sem_inc(items_ready, 1)

            def project(width, rhs, n):
                with pe.Fori(0, NT // TG) as i:
                    pe.wait_ge(stage_ready, 1)
                    pe.sem_inc(stage_ready, -1)
                    for q in range(TG):
                        last = t.transpose(ps[0:width, q * P:(q + 1) * P], stage[:, q * width:(q + 1) * width], ident[:])
                    last.then_inc(stage_mm, 1)
                    pe.wait_ge(xT_ready, 1)
                    pe.sem_inc(xT_ready, -1)
                    pe.sem_inc(in_ready, 1)
                    pe.wait_ge(proj_free, 1)
                    pe.sem_inc(proj_free, -1)
                    for q in range(TG):
                        o = 2 * BANK + q * 256
                        last = t.matmul(ps[:, o:o + n], xT[0:width, q * P:(q + 1) * P], rhs, start=True, stop=True)
                    last.then_inc(proj_mm, 1)
                pe.wait_ge(in_ready, 1)
                pe.sem_inc(in_ready, -1)

            pe.wait_ge(weights_in, 16 * N_WEIGHTS)
            pe.sem_inc(proj_free, 1)
            project(D, w_qkv[:], 3 * D)

            def rows_to_columns(rows=tmp_r, o=2 * BANK):
                pe.wait_ge(tr_ready, 1)
                pe.sem_inc(tr_ready, -1)
                for k in range(KB):
                    last = t.transpose(ps[:, o + k * P:o + (k + 1) * P], rows[:, k, :], ident[:])
                last.then_inc(tr_mm, 1)

            def carries_to_columns(o=0):
                pe.wait_ge(carry_ready, 1)
                pe.sem_inc(carry_ready, -1)
                for q in range(2):
                    for k in range(KB):
                        last = t.matmul(ps[:, o + q * KB + k:o + q * KB + k + 1], ends[0:1, q, k * P:(k + 1) * P],
                                        ones[0:1, 0:1], start=True, stop=True)
                last.then_inc(carry_mm, 1)

            pe.wait_ge(proj_free, 1)
            pe.sem_inc(proj_free, -1)
            for n in range(4):
                rows_to_columns()
            pe.wait_ge(ends_ready, 1)
            pe.sem_inc(ends_ready, -1)
            columns_to_rows(carry_c[:, 0:KB], carry_c[:, KB:2 * KB]).then_inc(ends_mm, 1)
            carries_to_columns()
            rows_to_columns()
            pe.wait_ge(parts_ready, 1)
            pe.sem_inc(parts_ready, -1)

            def zero(n_banks):
                for b in range(n_banks):
                    last = t.matmul(ps[:, b * BANK:(b + 1) * BANK], zeros_bf[0:1, 0:P], zeros_bf[:], start=True, stop=True)
                return last

            def hidden(gb):
                pe.wait_ge(ab_ready, 1)
                pe.sem_inc(ab_ready, -1)
                for s in range(3):
                    last = t.matmul(ps[:, HID + gb * BANK:HID + (gb + 1) * BANK], w_in3[:, s, :],
                                    attrs_b[:, gb, :], start=(s == 0), stop=(s == 2))
                last.then_inc(hid_mm, 1)

            def edge_weights(j, tiles):
                b = WQ + (j % 2) * BANK
                pe.wait_ge(wq_free, 1)
                pe.sem_inc(wq_free, -1)
                pe.wait_ge(ohn_ready, 1)
                pe.sem_inc(ohn_ready, -1)
                if j % 2 == 1:
                    pe.sem_inc(bd_free, 1)
                for i in range(G):
                    o = b + G * D + i * D
                    parts = part3[:, :, ds(tiles[i] * D, D)]
                    for s in range(3):
                        t.matmul(ps[:, o:o + D], oh_n[:, j, i * P:(i + 1) * P], parts[:, s, :],
                                 start=(s == 0), stop=(s == 2), skip_group_check=True)
                t.matmul(ps[:, b:b + G * D], ones_bf[:], b_out[:].rearrange("a g d -> a (g d)"), start=True, stop=False,
                         skip_group_check=True)
                pe.wait_ge(hs_ready, 1)
                pe.sem_inc(hs_ready, -1)
                for i in range(G):
                    last = t.matmul(ps[:, b + i * D:b + (i + 1) * D], hid_s[:, j % 2, i * P:(i + 1) * P], w_out[:],
                                    start=False, stop=True, skip_group_check=True)
                last.then_inc(wq_ready, 1)
                pe.sem_inc(hs_free, 1)

            def scatter0(j, tiles):
                pe.wait_ge(msg_ready, 1)
                pe.sem_inc(msg_ready, -1)
                for i in range(G):
                    for s in range(3):
                        last = t.matmul(ps[:, ds(tiles[i] * D, D)], oh_b[:, j, i * P:(i + 1) * P],
                                        top_half(msg3[:, j, s, i * D:(i + 1) * D]),
                                        start=False, stop=True, skip_group_check=True)
                last.then_inc(oh_free, 1)

            pe.sem_inc(bd_free, 2)
            pe.sem_inc(hs_free, 2)
            hidden(0)
            zero(4)
            for j in range(STEPS - 1):
                first = max(j - 2, 0)
                tiles = load_regs(ET.PE, t_row, first * G, (j - first + 1) * G, NT - 1)
                edge_weights(j, tiles[-G:])
                hidden((j + 1) % 2)
                if j >= 2:
                    scatter0(j - 2, tiles[:G])
            with pe.Fori(1, NB) as it:
                for j in range(STEPS):
                    tiles = load_regs(ET.PE, t_row, it * BODY + (j - 3) * G, 3 * G, NT - 1)
                    edge_weights((j - 1) % STEPS, tiles[-G:])
                    hidden(j % 2)
                    scatter0((j - 3) % STEPS, tiles[:G])
            tiles = load_regs(ET.PE, t_row, NI - 3 * G, 3 * G, NT - 1)
            edge_weights(STEPS - 1, tiles[-G:])
            pe.wait_ge(ab_ready, 1)
            pe.sem_inc(ab_ready, -1)
            for j in range(3):
                scatter0(j + 1, tiles[j * G:(j + 1) * G])

            pe.wait_ge(acc_free, 1)
            pe.sem_inc(acc_free, -1)
            pe.sem_inc(proj_free, 1)
            for layer in range(2):
                project(D if layer == 0 else P, w1x[:] if layer == 0 else w2x[:], H * C + 4)
                pe.wait_ge(parts_ready, 1)
                pe.sem_inc(parts_ready, -1)

                def select(c8, hb):
                    b = WQ + hb * BANK
                    pe.wait_ge(sel_free, 1)
                    pe.sem_inc(sel_free, -1)
                    pe.wait_ge(sel_oh, 1)
                    pe.sem_inc(sel_oh, -1)
                    pe.sem_inc(bc_free, 1)
                    tiles = load_regs(ET.PE, t_row, c8 * 8, 8, NT - 1)
                    for i in range(8):
                        terms = ps[:, b + i * H * NS:b + (i + 1) * H * NS].rearrange("p (h t) -> p h t", h=H)
                        for s in range(3):
                            t.matmul(terms[:, :, 0:NT], bc_s[:, hb, i * P:(i + 1) * P], as3[:, s, :, :],
                                     start=(s == 0), stop=(s == 2))
                        last = t.matmul(terms[:, :, NT:NS], oh_n8(hb)[:, i * P:(i + 1) * P],
                                        ad3[:, ds(tiles[i] * (H * 3), H * 3)].rearrange("p (h s) -> p h s", h=H),
                                        start=True, stop=True)
                    last.then_inc(sel_mm, 1)

                with pe.Fori(0, NB) as it:
                    for hb in range(2):
                        select(it * 2 + hb, hb)
                pe.wait_ge(sel_free, 2)
                pe.sem_inc(sel_free, -2)
                pe.wait_ge(lrow_ready, 1)
                pe.sem_inc(lrow_ready, -1)
                for h in range(H):
                    for k in range(KB):
                        last = t.transpose(ps[:, (2 * h) * BANK + k * P:(2 * h) * BANK + (k + 1) * P],
                                           l_e[:, h, k * P:(k + 1) * P], ident[:])
                    last.then_inc(lrow_mm, 1)
                pe.wait_ge(ends_ready, 1)
                pe.sem_inc(ends_ready, -1)
                columns_to_rows(carry_c[:, 0:KB], carry_c[:, KB:2 * KB]).then_inc(ends_mm, 1)
                carries_to_columns(CARRY)
                pe.wait_ge(ends_ready, 1)
                pe.sem_inc(ends_ready, -1)
                columns_to_rows(carry_c[:, 0:KB], carry_c[:, KB:2 * KB]).then_inc(ends_mm, 1)
                maxima_to_columns = lambda h: rows_to_columns(by_row(l_e[:, h, :]), MAX_AT)
                maxima_to_columns(0)
                carries_to_columns(CARRY)
                maxima_to_columns(1)
                for h in range(H):
                    pe.wait_ge(exp_ready, 1)
                    pe.sem_inc(exp_ready, -1)
                    if h:
                        pe.wait_ge(exp_out, 1)
                        pe.sem_inc(exp_out, -1)
                    for k in range(KB):
                        last = t.transpose(ps[:, EXP_AT + k * P:EXP_AT + (k + 1) * P], l_r[:, h, k * P:(k + 1) * P], ident[:])
                    last.then_inc(prow_mm, 1)
                pe.wait_ge(exp_out, 1)
                pe.sem_inc(exp_out, -1)
                pe.wait_ge(acc_free, 1)
                pe.sem_inc(acc_free, -1)
                zero(7)

                with pe.Fori(0, NB) as it:
                    for j in range(STEPS):
                        pe.wait_ge(msg_ready, 1)
                        pe.sem_inc(msg_ready, -1)
                        pe.sem_inc(ring_free, 1)
                        at = it * BODY + j * G
                        tiles = load_regs(ET.PE, t_row, at, G, NT - 1)
                        for i in range(G):
                            o = i * P
                            t.matmul(ps[:, ds(tiles[i] * P, P)], oh_e[:, j, o:o + P], msg[:, j, o:o + P],
                                     start=False, stop=True, skip_group_check=True)
                            last = t.matmul(ps[:, ds(tiles[i] * NX + SUMS, NX)], oh_e[:, j, o:o + P],
                                            ex[:, :, ds(at + i, 1)], start=False, stop=True, skip_group_check=True)
                        last.then_inc(oh_free, 1)
                pe.wait_ge(acc_free, 1)
                pe.sem_inc(acc_free, -1)


N_WEIGHTS = 27


def kernel(**inputs):
    import numpy as np
    import concourse.bacc as bacc
    from concourse.bass_utils import run_bass_kernel_spmd as run

    def rows(a, pad):
        full = np.full((NIP * P,), pad, a.dtype)
        full[:E] = a
        return full.reshape(NIP, P)

    a = {k: np.ascontiguousarray(v) for k, v in inputs.items()}
    attrs = np.zeros((PA - A_AT[0], EP), a["edge_attr_8"].dtype)
    for r in A_AT:
        attrs[r - A_AT[0]:][:F8, :E] = a["edge_attr_8"].T
        attrs[r - A_AT[0]:][F8:F, :E] = a["edge_attr_16"].T
    arrays = {"x": a["x"], "src_rows": rows(a["src"], 0), "dst_rows": rows(a["dst"], DST_PAD),
              "ew_rows": rows(a["edge_weight"], 0), "attrs": attrs}
    for k in ("W_rad1", "b_rad1", "W_rad2", "b_rad2", "W_sph1", "b_sph1", "W_sph2", "b_sph2", "Wq", "Wk", "Wv"):
        arrays[k] = a["L0_gnn_" + k]
    for k in ("W1", "as1", "ad1", "b1", "W2", "as2", "ad2", "b2"):
        arrays[k] = a["L1_gnn_" + k]
    nc = bacc.Bacc("TRN2", target_bir_lowering=False, num_devices=1)
    args = [nc.dram_tensor(k, v.shape, mybir.dt.from_np(v.dtype), kind="ExternalInput").ap() for k, v in arrays.items()]
    out = nc.dram_tensor("out", (N, D), mybir.dt.float32, kind="ExternalOutput").ap()
    gnn(nc, *args, out)
    r = run(nc, [arrays], core_ids=[0])
    return r.results[0]["out"]
```
